# Optimizing a Trainium2 kernel written in Bass

```python
import numpy as np
import jax
import jax.numpy as jnp

def _softmax(x, axis=-1):
    return jax.nn.softmax(x, axis=axis)

def _gelu(x):
    return jax.nn.gelu(x, approximate=True)

def _silu(x):
    return jax.nn.silu(x)

def _sigmoid(x):
    return jax.nn.sigmoid(x)

def _layernorm(x, axis=-1, eps=1e-05):
    m = jnp.mean(x, axis=axis, keepdims=True)
    v = jnp.var(x, axis=axis, keepdims=True)
    return (x - m) / jnp.sqrt(v + eps)

def _scatter_add(tgt, idx, src, axis=0):
    return tgt.at[idx].add(src)

def _segment_sum(src, seg, n):
    return jax.ops.segment_sum(src, seg, n)
kernel_name = 'mk_decoder_preln_d1_seqx_r4_3f988f'

def setup_inputs(seed: int=0):
    np.random.seed(seed)
    _w = jnp.asarray

    def _rec_inputs():
        import jax
        import jax.numpy as jnp
        _rk = jax.random.key(seed)
        x = 7.22e-05 + 1 * jax.random.normal(jax.random.fold_in(_rk, 1), (4, 512, 512), jnp.float32)
        _lenS = 512 - jax.random.randint(jax.random.fold_in(_rk, 7), (4,), 0, max(1, 512 // 4) + 1, jnp.int32)
        _lenS2 = 512 - jax.random.randint(jax.random.fold_in(_rk, 8), (4,), 0, max(1, 512 // 4) + 1, jnp.int32)
        _ctx_1024P = jax.random.normal(jax.random.fold_in(_rk, 11), (4, 16, 256), jnp.float32)
        _ctx_1024c = jax.random.dirichlet(jax.random.fold_in(_rk, 511), 0.3 * jnp.ones((16,), jnp.float32), (4, 512))
        _ctx_1024t = jnp.einsum('bsk,bkd->bsd', _ctx_1024c, _ctx_1024P)
        _ctx_1024t = _ctx_1024t * jax.lax.rsqrt(jnp.mean(jnp.square(_ctx_1024t)) + 1e-12) * 0.953939
        ctx_1024 = 2.81802e-05 + 1.00001 * (_ctx_1024t + 0.3 * jax.random.normal(jax.random.fold_in(_rk, 611), (4, 512, 256), jnp.float32))
        return (x, ctx_1024)
    x, ctx_1024 = _rec_inputs()

    def _L0_attn_setup():
        import jax, jax.numpy as jnp
        import numpy as np
        HEADS = 16
        key = jax.random.key(seed)
        ks = jax.random.split(key, 5)
        B, T, D = (2, 512, 512)
        s = 0.02
        return {'x': jax.random.normal(ks[0], (B, T, D), dtype=jnp.float32), 'Wq': jax.random.normal(ks[1], (D, D), dtype=jnp.float32) * s, 'Wk': jax.random.normal(ks[2], (D, D), dtype=jnp.float32) * s, 'Wv': jax.random.normal(ks[3], (D, D), dtype=jnp.float32) * s, 'Wo': jax.random.normal(ks[4], (D, D), dtype=jnp.float32) * s}
    _L0_attn_all = _L0_attn_setup()
    _L0_attn_in = {k: v for k, v in _L0_attn_all.items() if k in ('Wq', 'Wk', 'Wv', 'Wo')}
    del _L0_attn_all

    def _L0_xattn_setup():
        import jax, jax.numpy as jnp
        import numpy as np
        key = jax.random.key(seed)
        ks = jax.random.split(key, 6)
        B, L, N, C, D = (8, 128, 512, 256, 128)
        return {'teacher_logits': jax.random.normal(ks[0], (B, L, N), dtype=jnp.float32), 'teacher_features': jax.random.normal(ks[1], (B, N, C), dtype=jnp.float32), 'Wq': jax.random.normal(ks[2], (D, C), dtype=jnp.float32) * (1.0 / np.sqrt(C)), 'bq': jnp.zeros((D,), dtype=jnp.float32), 'Wk': jax.random.normal(ks[3], (D, C), dtype=jnp.float32) * (1.0 / np.sqrt(C)), 'bk': jnp.zeros((D,), dtype=jnp.float32)}
    _L0_xattn_all = _L0_xattn_setup()
    _L0_xattn_in = {k: v for k, v in _L0_xattn_all.items() if k in ('Wq', 'bq', 'Wk', 'bk')}
    del _L0_xattn_all

    def _L0_ffn_setup():
        import jax, jax.numpy as jnp
        import numpy as np
        BLOCK_SIZE = 32
        HIDDEN_SIZE = 512
        MLP_DIM = 4096
        NVFP4_LUT = jnp.array([0.0, 0.5, 1.0, 1.5, 2.0, 3.0, 4.0, 6.0, 0.0, -0.5, -1.0, -1.5, -2.0, -3.0, -4.0, -6.0], dtype=jnp.float32)

        def dequant_nvfp4(W_packed, scales, block=BLOCK_SIZE):
            N = W_packed.shape[0]
            low = W_packed & 15
            high = W_packed >> 4 & 15
            idx = jnp.stack([low, high], axis=-1).reshape(N, -1)
            vals = NVFP4_LUT[idx]
            K = vals.shape[1]
            vals = vals.reshape(N, K // block, block) * scales[:, :, None]
            return vals.reshape(N, K)
        key = jax.random.key(seed)
        ks = jax.random.split(key, 7)
        x = jax.random.normal(ks[0], (4, 32, HIDDEN_SIZE), dtype=jnp.float32)
        gate_W_packed = jax.random.randint(ks[1], (MLP_DIM, HIDDEN_SIZE // 2), 0, 64, dtype=jnp.int32)
        gate_scales = jax.random.uniform(ks[2], (MLP_DIM, HIDDEN_SIZE // BLOCK_SIZE), dtype=jnp.float32) * 0.1 + 0.001
        up_W_packed = jax.random.randint(ks[3], (MLP_DIM, HIDDEN_SIZE // 2), 0, 64, dtype=jnp.int32)
        up_scales = jax.random.uniform(ks[4], (MLP_DIM, HIDDEN_SIZE // BLOCK_SIZE), dtype=jnp.float32) * 0.1 + 0.001
        down_W_packed = jax.random.randint(ks[5], (HIDDEN_SIZE, MLP_DIM // 2), 0, 64, dtype=jnp.int32)
        down_scales = jax.random.uniform(ks[6], (HIDDEN_SIZE, MLP_DIM // BLOCK_SIZE), dtype=jnp.float32) * 0.1 + 0.001
        return {'x': x, 'gate_W_packed': gate_W_packed, 'gate_scales': gate_scales, 'up_W_packed': up_W_packed, 'up_scales': up_scales, 'down_W_packed': down_W_packed, 'down_scales': down_scales}
    _L0_ffn_all = _L0_ffn_setup()
    _L0_ffn_in = {k: v for k, v in _L0_ffn_all.items() if k in ('gate_W_packed', 'gate_scales', 'up_W_packed', 'up_scales', 'down_W_packed', 'down_scales')}
    del _L0_ffn_all
    return {'x': x, 'ctx_1024': ctx_1024, 'L0_attn_Wq': _L0_attn_in['Wq'], 'L0_attn_Wk': _L0_attn_in['Wk'], 'L0_attn_Wv': _L0_attn_in['Wv'], 'L0_attn_Wo': _L0_attn_in['Wo'], 'L0_xattn_Wq': _L0_xattn_in['Wq'], 'L0_xattn_bq': _L0_xattn_in['bq'], 'L0_xattn_Wk': _L0_xattn_in['Wk'], 'L0_xattn_bk': _L0_xattn_in['bk'], 'L0_ffn_gate_W_packed': _L0_ffn_in['gate_W_packed'], 'L0_ffn_gate_scales': _L0_ffn_in['gate_scales'], 'L0_ffn_up_W_packed': _L0_ffn_in['up_W_packed'], 'L0_ffn_up_scales': _L0_ffn_in['up_scales'], 'L0_ffn_down_W_packed': _L0_ffn_in['down_W_packed'], 'L0_ffn_down_scales': _L0_ffn_in['down_scales']}

def reference(x, ctx_1024, L0_attn_Wq, L0_attn_Wk, L0_attn_Wv, L0_attn_Wo, L0_xattn_Wq, L0_xattn_bq, L0_xattn_Wk, L0_xattn_bk, L0_ffn_gate_W_packed, L0_ffn_gate_scales, L0_ffn_up_W_packed, L0_ffn_up_scales, L0_ffn_down_W_packed, L0_ffn_down_scales):
    import jax
    import jax.numpy as jnp

    def _L0_attn_ref(x, Wq, Wk, Wv, Wo):
        import jax, jax.numpy as jnp
        import numpy as np
        HEADS = 16
        B, T, _ = x.shape
        H = HEADS
        Dh = Wq.shape[1] // H
        q = (x @ Wq).reshape(B, T, H, Dh)
        k = (x @ Wk).reshape(B, T, H, Dh)
        v = (x @ Wv).reshape(B, T, H, Dh)
        scores = jnp.einsum('bthd,bshd->bhts', q, k)
        mask = jnp.tril(jnp.ones((T, T), dtype=scores.dtype))
        scores = scores * mask
        attn = jax.nn.softmax(scores / T ** 0.5, axis=-1)
        out = jnp.einsum('bhts,bshd->bthd', attn, v).reshape(B, T, H * Dh)
        return out @ Wo

    def _L0_xattn_ref(teacher_logits, teacher_features, Wq, bq, Wk, bk):
        import jax, jax.numpy as jnp
        import numpy as np
        query = jnp.einsum('bnc,dc->bnd', teacher_features, Wq) + bq
        key = jnp.einsum('bnc,dc->bnd', teacher_features, Wk) + bk
        energy = jnp.einsum('bnd,bmd->bnm', query, key)
        attention = jax.nn.softmax(energy, axis=-1)
        x_m = jnp.einsum('bln,bmn->blm', teacher_logits, attention)
        return x_m

    def _L0_ffn_ref(x, gate_W_packed, gate_scales, up_W_packed, up_scales, down_W_packed, down_scales):
        import jax, jax.numpy as jnp
        import numpy as np
        BLOCK_SIZE = 32
        HIDDEN_SIZE = 512
        MLP_DIM = 4096
        NVFP4_LUT = jnp.array([0.0, 0.5, 1.0, 1.5, 2.0, 3.0, 4.0, 6.0, 0.0, -0.5, -1.0, -1.5, -2.0, -3.0, -4.0, -6.0], dtype=jnp.float32)

        def dequant_nvfp4(W_packed, scales, block=BLOCK_SIZE):
            N = W_packed.shape[0]
            low = W_packed & 15
            high = W_packed >> 4 & 15
            idx = jnp.stack([low, high], axis=-1).reshape(N, -1)
            vals = NVFP4_LUT[idx]
            K = vals.shape[1]
            vals = vals.reshape(N, K // block, block) * scales[:, :, None]
            return vals.reshape(N, K)
        B, S, H = x.shape
        xt = x.reshape(B * S, H)
        Wg = dequant_nvfp4(gate_W_packed, gate_scales)
        Wu = dequant_nvfp4(up_W_packed, up_scales)
        Wd = dequant_nvfp4(down_W_packed, down_scales)
        gate = jnp.einsum('th,nh->tn', xt, Wg)
        up = jnp.einsum('th,nh->tn', xt, Wu)
        gelu = jnp.tanh(0.7978845608028654 * (gate + 0.044715 * gate ** 3)) * gate * 0.5 + gate * 0.5
        inter = gelu * up
        out = jnp.einsum('tn,hn->th', inter, Wd)
        return out.reshape(B, S, H)
    x = x + _L0_attn_ref(_layernorm(x, axis=-1), L0_attn_Wq, L0_attn_Wk, L0_attn_Wv, L0_attn_Wo)
    x = x + _L0_xattn_ref(_layernorm(x, axis=-1), ctx_1024, L0_xattn_Wq, L0_xattn_bq, L0_xattn_Wk, L0_xattn_bk)
    x = x + _L0_ffn_ref(_layernorm(x, axis=-1), L0_ffn_gate_W_packed, L0_ffn_gate_scales, L0_ffn_up_W_packed, L0_ffn_up_scales, L0_ffn_down_W_packed, L0_ffn_down_scales)
    return x

_drawn_inputs = setup_inputs


def setup_inputs(seed=0):
    import zlib

    import numpy as np

    out = dict(_drawn_inputs(seed))
    spreads = {'L0_xattn_bq': (0.0, 0.1), 'L0_xattn_bk': (0.0, 0.8)}
    factors = {'L0_attn_Wq': 8.0, 'L0_attn_Wk': 8.0, 'L0_attn_Wv': 5.552, 'L0_attn_Wo': 4.811}
    for name, (base, spread) in spreads.items():
        noise = np.random.default_rng([zlib.crc32(name.encode()), seed]).standard_normal(out[name].shape)
        drawn = base * np.exp(spread * noise) if base else spread * noise
        out[name] = jnp.asarray(drawn.astype(out[name].dtype))
    for name, factor in factors.items():
        out[name] = (out[name] * factor).astype(out[name].dtype)
    return out
```

```python
from contextlib import ExitStack

import numpy as np

import concourse.bass as bass
from concourse import mybir

F32 = mybir.dt.float32
F16 = mybir.dt.float16
I32 = mybir.dt.int32
U32 = mybir.dt.uint32
I16 = mybir.dt.int16
U8 = mybir.dt.uint8
ALU = mybir.AluOpType
ACT = mybir.ActivationFunctionType
AX = mybir.AxisListType
RMAX = bass.bass_isa.ReduceOp.max

P = 128
B, T, D = 4, 512, 512
HEADS, DH = 16, 32
C, DX = 256, 128
F = 4096
QBLOCK = 32
TT = T // P
KT = D // P
HG = HEADS // 4
UNITS = HG * TT
NB = F // 256
HALF = 768
EPS = 1e-5

XS = 2.0 ** 11
QS = 2.0 ** -18
AS = 2.0 ** 14
TOP = 127 + 12
CAP = 127 + 60
LUT = 2.0 ** 14
NEG = -3.0e38

WEIGHTS = ("q", "k", "v", "o")
SG, SU, SD = 4, 5, 6


class Steps:

    def __init__(self, eng, sem, base, per):
        self.eng, self.sem, self.base, self.per, self.k = eng, sem, base, per, 0

    def mark(self, ins):
        ins.then_inc(self.sem, 1)
        self.k += 1

    def settle(self):
        self.eng.wait_ge(self.sem, self.base + self.k)

    def end(self):
        assert self.k == self.per, (self.k, self.per)


def decoder_layer(nc, x, ctx_1024, Wq, Wk, Wv, Wo, xWq, xbq, xWk, xbk, gate_p, gate_s, up_p, up_s, down_p, down_s, out):
    with ExitStack() as ctx:
        def sem(name):
            return ctx.enter_context(nc.semaphore(name))

        def psum(name, shape, dt):
            return ctx.enter_context(nc.psum_tensor(name, shape, dt))

        def keep(name, shape, dt):
            return ctx.enter_context(nc.sbuf_tensor(name, shape, dt))

        packed_t = nc.dram_tensor("packed_t", (2 * NB, P, HALF), I16, kind="Internal").ap()
        scale_t = nc.dram_tensor("scale_t", (2 * NB, 8, HALF), F32, kind="Internal").ap()
        xf_dram = nc.dram_tensor("xf_dram", (B, P, 2 * KT * T), F16, kind="Internal").ap()

        bank = [psum(f"bank{i}", [P, 512], F32) for i in range(8)]
        X = keep("X", [P, B * TT, D], F32)
        fac = keep("fac", [P, 7], F32)
        ifac = keep("ifac", [P, 7], F32)
        col = keep("col", [P, 12], F32)
        C_EXP, C_NEXP, C_O, C_G, C_I, C_OUT, C_SG, C_SU, C_SD = (col[:, i:i + 1] for i in range(9))
        tmpc = keep("tmpc", [P, 4], F32)

        first = ExitStack()

        def sb(name, shape, dt):
            return first.enter_context(nc.sbuf_tensor(name, shape, dt))

        stack = sb("stack", [P, 2, HEADS, T], F16)
        w_raw = stack[:].rearrange("p a h t -> p (a h t)").bitcast(F32).rearrange("p (w k n) -> p w k n", w=4, k=KT)
        w_split = sb("w_split", [P, 2, 4, KT, D], F16)
        xn = sb("xn", [P, TT, D], F32)
        xt = sb("xt", [P, 2, KT, T], F16)
        qk = sb("qk", [P, 4, 2, T], F16)
        V = sb("V", [P, TT, D], F32)
        v_tail = sb("v_tail", [P, 2, D], F32)
        prob = sb("prob", [P, 2, 4, T], F32)
        prob_t = sb("prob_t", [P, 2, 4, T], F32)
        o_t = sb("o_t", [P, 2, HG, T], F16)
        att_t = sb("att_t", [P, 2, KT, T], F16)
        c_in = sb("c_in", [P, TT, C], F32)
        c_t = prob_t[:, 0, 0:2, :]
        qk_x = prob_t[:, 1, 0:2, :]
        e_p = prob[:, 0, :, :]
        xw = sb("xw", [P, 2, C], F32)
        xw_t = sb("xw_t", [P, 2, 2, DX], F32)
        xb = sb("xb", [P, 2], F32)
        mask = sb("mask", [P, 5 * P], F32)
        ident = sb("ident", [P, P], F32)
        ident16 = sb("ident16", [P, P], F16)
        ones = V[:].rearrange("p t d -> p (t d)")[:, 0:5 * P]
        o_raw = o_t[:].rearrange("p a h t -> p (a h t)").bitcast(F32)
        gs_in = o_raw[:, 0:1024].rearrange("p (i n k) -> p i n k", i=2, k=D // QBLOCK)
        ds_in = o_raw[:, 1024:1536].rearrange("p (t k) -> p t k", t=KT)
        gu_st = [prob[0:16].rearrange("p a j t -> p (a j t)"), prob_t[0:16].rearrange("p a j t -> p (a j t)")]
        d_st = v_tail[:, 0]
        most = sb("most", [P, 7], F32)
        most_all = sb("most_all", [P, 7], F32)
        expo = sb("expo", [P, 2, 7], I32)
        pk_in = sb("pk_in", [P, 6, C], I32)
        pk_16 = sb("pk_16", [P, 6, C], F16)
        pk_t = sb("pk_t", [P, 2, HALF], I16)
        st6 = sb("st6", [P, TT, 6], F32)
        mv = sb("mv", [P, TT, 2], F32)
        var = sb("var", [P, TT], F32)
        rs = sb("rs", [P, 2, TT], F32)
        rsi = sb("rsi", [P, TT], I32)
        mx = sb("mx", [P, 2, 4], F32)
        nmx = sb("nmx", [P, 2, 4], F32)
        den = sb("den", [P, 2, 4], F32)
        rden = sb("rden", [P, 2, 4], F32)
        x_nm = sb("x_nm", [P, 4], F32)
        x_den = sb("x_den", [P, 4], F32)
        x_rden = sb("x_rden", [P, 4], F32)
        first.close()

        second = ExitStack()

        def sb2(name, shape, dt):
            return second.enter_context(nc.sbuf_tensor(name, shape, dt))

        ring = sb2("ring", [P, 2, 8, 2, HALF], F16)
        xf = sb2("xf", [P, 2, 2, KT, T], F16)
        pk_in2 = sb2("pk_in2", [P, 2, HALF], I16)
        sc_in = sb2("sc_in", [P, 2, HALF], F32)
        bits = sb2("bits", [P, 2, HALF // 2], U32)
        codes = sb2("codes", [P, 2, HALF // 2], U32)
        w_full = sb2("w_full", [P, 2, HALF], F32)
        g_sb = sb2("g_sb", [P, 2, T], F32)
        sq = sb2("sq", [P, 2, T], F32)
        cube = sb2("cube", [P, 2, T], F32)
        th = sb2("th", [P, 2, T], F32)
        gel = sb2("gel", [P, 2, T], F32)
        inter = sb2("inter", [P, 2, T], F32)
        hid = sb2("hid", [P, 2, 2, T], F16)
        second.close()

        ld_w, ld_s, ld_x0, ld_x, ld_small = (sem(n) for n in ("ld_w", "ld_s", "ld_x0", "ld_x", "ld_small"))
        ld_ctx, ld_pk = sem("ld_ctx"), sem("ld_pk")
        const_ones, const_done = sem("const_ones"), sem("const_done")
        most_done, all_done, fac_step = sem("most_done"), sem("all_done"), sem("fac_step")
        w_hi, w_lo = sem("w_hi"), sem("w_lo")
        st_full, st_out, st_stored = sem("st_full"), sem("st_out"), sem("st_stored")
        xw_full, xw_done = sem("xw_full"), sem("xw_done")
        ln_step = [sem(f"ln{i}_step") for i in range(3)]
        ln_done = [sem(f"ln{i}_done") for i in range(3)]
        spread_full = [sem(f"spread{i}_full") for i in range(3)]
        spread_hi = [sem(f"spread{i}_hi") for i in range(3)]
        spread_lo = [sem(f"spread{i}_lo") for i in range(3)]
        qkv_full, qk_hi, qk_lo, v_out, vt_step = (sem(n) for n in ("qkv_full", "qk_hi", "qk_lo", "v_out", "vt_step"))
        stacked = [sem(f"stacked{i}") for i in range(4)]
        s_full, max_done, shift_done, exp_done = (sem(n) for n in ("s_full", "max_done", "shift_done", "exp_done"))
        den_step, norm_done, t_full = sem("den_step"), sem("norm_done"), sem("t_full")
        pt_act, pt_dve, av_done, o_hi, o_lo = (sem(n) for n in ("pt_act", "pt_dve", "av_done", "o_hi", "o_lo"))
        wo_full, x1_done, mix_full, x2_done = (sem(n) for n in ("wo_full", "x1_done", "mix_full", "x2_done"))
        ct_full, ct_done, qkx_full, qkx_done = (sem(n) for n in ("ct_full", "ct_done", "qkx_full", "qkx_done"))
        en_full, en_max, en_exp, en_step, att_full, att_hi, att_lo = (
            sem(n) for n in ("en_full", "en_max", "en_exp", "en_step", "att_full", "att_hi", "att_lo"))
        pk_conv, pk_full, pk_out0, pk_out1, pk_stored = (sem(n) for n in ("pk_conv", "pk_full", "pk_out0", "pk_out1", "pk_stored"))
        xf_stored = sem("xf_stored")
        in_pk, in_xf = [sem("in_pk0"), sem("in_pk1")], [sem("in_xf0"), sem("in_xf1")]
        dq_step, dq_full, dq_hi, dq_lo = (sem(n) for n in ("dq_step", "dq_full", "dq_hi", "dq_lo"))
        g_full, u_full, g_out, sq_out, cube_out, th_out = (sem(n) for n in ("g_full", "u_full", "g_out", "sq_out", "cube_out", "th_out"))
        gel_out, int_out, hid_hi, hid_lo, down_done, acc_full, acc_out = (
            sem(n) for n in ("gel_out", "int_out", "hid_hi", "hid_lo", "down_done", "acc_full", "acc_out"))
        out_stored, passed = sem("out_stored"), sem("passed")

        LN_STEPS = 4 + 4 + 3 + 9
        DEN_STEPS = {0: 2, 1: 2, 2: 1, 3: 1}
        UNIT_DEN = [sum(DEN_STEPS[v % TT] for v in range(u)) for u in range(UNITS + 1)]
        wide = [min(T, (i + 2) * P) for i in range(TT)]

        def alone(eng, sem, value):
            eng.wait_ge(sem, value)
            eng.sem_inc(passed, 1)

        def walk(body):
            def run(eng):
                with eng.Fori(0, B - 1) as n:
                    body(n, False)
                body(B - 1, True)
            return run

        block = ctx.enter_context(nc.Block())

        @block.sync
        def _(sp):
            sp.dma_start(X[:, 0:TT, :], x[0].rearrange("(t p) d -> p t d", p=P)).then_inc(ld_x0, 16)
            for w, src in enumerate((Wq, Wk, Wv, Wo)):
                sp.dma_start(w_raw[:, w], src.rearrange("(k p) n -> p k n", p=P)).then_inc(ld_w, 16)
            for i, src in enumerate((gate_s, up_s)):
                sp.dma_start(gs_in[:, i].rearrange("p (n r) k -> p n (r k)", r=2),
                             src.rearrange("(n p r) k -> p n (r k)", p=P, r=2)).then_inc(ld_s, 16)
            sp.dma_start(ds_in[:], down_s.rearrange("(t p) k -> p t k", p=P)).then_inc(ld_s, 16)
            for i, (w, bv) in enumerate(((xWq, xbq), (xWk, xbk))):
                sp.dma_start(xw[:, i], w).then_inc(ld_small, 16)
                sp.dma_start(xb[:, i:i + 1], bv.rearrange("(p a) -> p a", a=1)).then_inc(ld_small, 16)
            for b in range(1, B):
                sp.dma_start(X[:, b * TT:(b + 1) * TT, :], x[b].rearrange("(t p) d -> p t d", p=P)).then_inc(ld_x, 16)

            def load_ctx(n):
                if not isinstance(n, int) or n > 0:
                    sp.wait_ge(ct_full, n * 2)
                sp.dma_start(c_in[:], ctx_1024[n].rearrange("(t p) c -> p t c", p=P) if isinstance(n, int)
                             else ctx_1024[bass.ds(n, 1)].rearrange("a (t p) c -> p (a t) c", p=P)).then_inc(ld_ctx, 16)

            def stack_heads(n):
                for g in range(2 * HG):
                    c, which = g // 2, g % 2
                    sp.wait_ge(qk_lo, n * 2 * HG + g + 1)
                    for j in range(4):
                        for part in range(4):
                            hl = part % 2 if which == 0 else part // 2
                            sp.dma_start(stack[32 * part:32 * part + 32, which, 4 * c + j, :],
                                         qk[32 * j:32 * j + 32, g % 4, hl, :]).then_inc(stacked[g % 4], 16)

            load_ctx(0)
            for i in range(2):
                sp.wait_ge(st_out, 8 * (i + 1))
                for kk in range(2):
                    hb, piece = (0, kk) if i == 0 else (kk, 2 * (1 - kk))
                    dst = scale_t.rearrange("(n a) k c -> k n a c", a=2)[:, :, hb, 256 * piece:256 * piece + 256]
                    sp.dma_start(dst, gu_st[i][8 * kk:8 * kk + 8, :].rearrange("k (n c) -> k n c", n=NB)).then_inc(st_stored, 16)
            sp.wait_ge(st_out, 17)
            for nb in range(NB):
                sp.dma_start(scale_t[2 * nb + 1, :, 256:768], d_st[8 * nb:8 * nb + 8, :]).then_inc(st_stored, 16)
            stack_heads(0)

            def body(n, last):
                if not last:
                    load_ctx(n + 1)
                    stack_heads(n + 1)
                for r in range(NB // B):
                    nb = n * (NB // B) + r
                    if r > 0 or not isinstance(n, int) or n > 0:
                        pass
                    sp.wait_ge(pk_conv, nb)
                    for i, src in enumerate((gate_p, up_p)):
                        rows = src.rearrange("(n p r) w -> n p r w", p=P, r=2)
                        sp.dma_start(pk_in[:, 2 * i:2 * i + 2, :], rows[bass.ds(nb, 1)].rearrange("a p r w -> p (a r) w")).then_inc(ld_pk, 16)
                    cols = down_p.rearrange("(t p) (n w) -> n p t w", p=P, w=P)
                    sp.dma_start(pk_in[:, 4:6, :].rearrange("p a (b w) -> p (a b) w", w=P),
                                 cols[bass.ds(nb, 1)].rearrange("a p t w -> p (a t) w")).then_inc(ld_pk, 16)
                    sp.wait_ge(pk_out0, nb + 1)
                    sp.dma_start(packed_t[bass.ds(2 * nb, 1)].rearrange("a p c -> p (a c)"), pk_t[:, 0]).then_inc(pk_stored, 16)
                    sp.wait_ge(pk_out1, nb + 1)
                    sp.dma_start(packed_t[bass.ds(2 * nb + 1, 1)].rearrange("a p c -> p (a c)"), pk_t[:, 1]).then_inc(pk_stored, 16)
                sp.wait_ge(spread_lo[2], (n + 1) * KT)
                sp.dma_start(xf_dram[bass.ds(n, 1)].rearrange("a p c -> p (a c)"),
                             xt[:].rearrange("p a k t -> p (a k t)")).then_inc(xf_stored, 16)

            walk(body)(sp)

            sp.wait_ge(xf_stored, 16 * B)
            sp.wait_ge(pk_stored, 16 * 2 * NB)
            sp.wait_ge(st_stored, 16 * (4 + NB))

            def load_half(hb, slot, ready):
                sp.dma_start(pk_in2[:, slot], packed_t[bass.ds(hb, 1)].rearrange("a p c -> p (a c)")).then_inc(in_pk[ready], 16)
                rows = scale_t[bass.ds(hb, 1)]
                sp.dma_start(sc_in[:, slot], bass.AP(rows.tensor, rows.offset, [[HALF, 8], [0, 16], [1, HALF]])).then_inc(in_pk[ready], 16)

            def load_xf(b, slot, ready):
                sp.dma_start(xf[:, slot].rearrange("p a k t -> p (a k t)"),
                             xf_dram[bass.ds(b, 1)].rearrange("a p c -> p (a c)")).then_inc(in_xf[ready], 16)

            load_xf(0, 0, 0)
            for hb in range(4):
                if hb >= 2:
                    sp.wait_ge(dq_full, hb - 1)
                load_half(hb, hb % 2, hb % 2)

            def mlp_loads(i2, odd, dequant, nxt):
                it = 2 * i2 + odd
                if dequant:
                    sp.wait_ge(dq_full, it + 3)
                    load_half(it + 4, odd, odd)
                if nxt:
                    if not isinstance(it, int) or it > 0:
                        sp.wait_ge(down_done, 4 * it - 1 + 1)
                    load_xf((it + 1) % B, 1 - odd, 1 - odd)

            def store(it):
                sp.wait_ge(acc_out, it + 1)
                sp.dma_start(out[it % B].rearrange("(t p) d -> p t d", p=P), X[:, (it % B) * TT:(it % B + 1) * TT, :]).then_inc(out_stored, 16)

            mlp_loads(0, 0, True, True)
            mlp_loads(0, 1, True, True)
            with sp.Fori(1, 14) as i2:
                mlp_loads(i2, 0, True, True)
                mlp_loads(i2, 1, True, True)
            for it in range(28, 32):
                mlp_loads(it // 2, it % 2, False, it < 31)
                if it > 28:
                    store(it - 1)
            store(31)
            sp.wait_ge(out_stored, 16 * B)

        @block.gpsimd
        def _(pool):
            nc.gpsimd.memset(ones[:], 1.0).then_inc(const_ones, 1)
            pool.wait_ge(const_ones, 1)
            nc.gpsimd.affine_select(out=mask[:], in_=ones[:], compare_op=ALU.is_ge, fill=0.0, base=3 * P,
                                    pattern=[[-1, 5 * P]], channel_multiplier=1).then_inc(const_done, 1)
            nc.gpsimd.affine_select(out=ident[:], in_=ones[:, 0:P], compare_op=ALU.is_equal, fill=0.0, base=0,
                                    pattern=[[-1, P]], channel_multiplier=1).then_inc(const_done, 1)
            nc.gpsimd.affine_select(out=ident16[:], in_=ones[:, 0:P], compare_op=ALU.is_equal, fill=0.0, base=0,
                                    pattern=[[-1, P]], channel_multiplier=1).then_inc(const_done, 1)
            pool.wait_ge(most_done, 7)
            nc.gpsimd.partition_all_reduce(most_all[:], most[:], P, RMAX).then_inc(all_done, 1)

            def value_sums(n):
                pool.wait_ge(v_out, n * TT + TT)
                nc.gpsimd.tensor_tensor(v_tail[:, 1], V[:, 2], V[:, 3], ALU.add).then_inc(vt_step, 1)
                pool.wait_ge(vt_step, n * 2 + 1)
                nc.gpsimd.tensor_tensor(v_tail[:, 0], v_tail[:, 1], V[:, 1], ALU.add).then_inc(vt_step, 1)

            pool.wait_ge(st_stored, 16 * (4 + NB))
            value_sums(0)

            def body(n, last):
                if not last:
                    value_sums(n + 1)
                for r in range(NB // B):
                    nb = n * (NB // B) + r
                    pool.wait_ge(ld_pk, (nb + 1) * 48)
                    alone(pool, pk_full, 2 * nb)
                    nc.gpsimd.tensor_copy(pk_16[:].rearrange("p a w -> p (a w)"),
                                          pk_in[:].rearrange("p a w -> p (a w)").bitcast(U8)
                                          .rearrange("p (c four) -> p c four", four=4)[:, :, 0]).then_inc(pk_conv, 1)

            walk(body)(pool)

        @block.tensor
        def _(pe):
            def three(o, lhs, rhs, first, stop):
                pe.matmul(o, lhs(0), rhs(0), start=first, stop=False)
                pe.matmul(o, lhs(0), rhs(1), start=False, stop=False)
                return pe.matmul(o, lhs(1), rhs(0), start=False, stop=stop)

            def spread(st, n, banks):
                for k in range(KT):
                    for t in range(TT):
                        if st < 2:
                            src = xn[:, t, P * k:P * k + P]
                        else:
                            src = xn[:, t, 256 * (k // 2) + k % 2:256 * (k // 2) + 256:2]
                        mm = pe.transpose(bank[banks + k][:, P * t:P * t + P], src, ident[:])
                    mm.then_inc(spread_full[st], 1)

            def qkv(n):
                pe.wait_ge(spread_lo[0], n * KT + KT)
                for g in range(12):
                    bk = bank[g % 4]
                    if g >= 4:
                        pe.wait_ge(qk_lo, n * 8 + min(g - 3, 8))
                    for k in range(KT):
                        if g < 8:
                            w, c = g % 2, g // 2
                            mm = three(bk[:], lambda a: w_split[:, a, w, k, P * c:P * c + P], lambda a: xt[:, a, k, :], k == 0, k == KT - 1)
                        else:
                            s = g - 8
                            mm = three(bk[:], lambda a: xt[:, a, k, P * s:P * s + P], lambda a: w_split[:, a, 2, k, :], k == 0, k == KT - 1)
                    mm.then_inc(qkv_full, 1)

            def scores(n, u):
                hg, i = u // TT, u % TT
                if i == 0:
                    for g in (2 * hg, 2 * hg + 1):
                        pe.wait_ge(stacked[g % 4], n * 512 + 256 * (g // 4) + 256)
                for j in range(4):
                    if u > 0:
                        pe.wait_ge(exp_done, n * 4 * UNITS + 4 * (u - 1) + j + 1)
                    h = 4 * hg + j
                    pe.matmul(bank[j][:, 0:wide[i]], stack[:, 0, h, P * i:P * i + P], stack[:, 1, h, 0:wide[i]],
                              start=True, stop=True).then_inc(s_full, 1)

            def turn(n, u):
                i = u % TT
                for j in range(4):
                    pe.wait_ge(norm_done, n * 4 * UNITS + 4 * u + j + 1)
                    if j < 2 and u == 0:
                        pass
                    elif j == 1:
                        pe.wait_ge(pt_dve, n * UNITS + u)
                    elif j == 0:
                        pe.wait_ge(pt_act, n * 3 * UNITS + 3 * u)
                    else:
                        pe.wait_ge(pt_act, n * 3 * UNITS + 3 * u + j - 1)
                    for k in range(wide[i] // P):
                        mm = pe.transpose(bank[4 + j % 2][:, P * k:P * k + P], prob[:, u % 2, j, P * k:P * k + P], ident[:])
                    mm.then_inc(t_full, 1)

            def values(n, u):
                hg, i = u // TT, u % TT
                pe.wait_ge(pt_act, n * 3 * UNITS + 3 * u + 3)
                pe.wait_ge(pt_dve, n * UNITS + u + 1)
                if u == 0:
                    pe.wait_ge(vt_step, n * 2 + 2)
                if i == 0 and hg >= 2:
                    pe.wait_ge(o_lo, n * HG + hg - 1)
                blocks = wide[i] // P
                for k in range(blocks):
                    v = v_tail[:, i, :] if i < 2 and k == blocks - 1 else V[:, k, :]
                    for j in range(4):
                        h = 4 * hg + j
                        mm = pe.matmul(bank[6 + hg % 2][32 * j:32 * j + 32, P * i:P * i + P], v[:, DH * h:DH * h + DH],
                                       prob_t[:, u % 2, j, P * k:P * k + P], start=(k == 0), stop=(k == blocks - 1))
                mm.then_inc(av_done, 1)

            def out_proj(n):
                pe.wait_ge(o_lo, n * HG + HG)
                for t in range(TT):
                    for k in range(KT):
                        mm = three(bank[4 + t][:], lambda a: o_t[:, a, k, P * t:P * t + P], lambda a: w_split[:, a, 3, k, :], k == 0, k == KT - 1)
                    mm.then_inc(wo_full, 1)

            def mix(n):
                pe.wait_ge(spread_lo[1], n * KT + KT)
                pe.wait_ge(att_lo, n * KT + KT)
                for t in range(TT):
                    for k in range(KT):
                        mm = three(bank[t][:], lambda a: xt[:, a, k, P * t:P * t + P], lambda a: att_t[:, a, k, :], k == 0, k == KT - 1)
                    mm.then_inc(mix_full, 1)

            def context(n):
                pe.wait_ge(ld_ctx, n * 16 + 16)
                for cc in range(2):
                    for t in range(TT):
                        mm = pe.transpose(bank[4 + cc][:, P * t:P * t + P], c_in[:, t, P * cc:P * cc + P], ident[:])
                    mm.then_inc(ct_full, 1)
                pe.wait_ge(ct_done, n * 2 + 2)
                for i in range(2):
                    for cc in range(2):
                        mm = pe.matmul(bank[6 + i][:], xw_t[:, cc, i, :], c_t[:, cc, :], start=(cc == 0), stop=(cc == 1))
                    mm.then_inc(qkx_full, 1)
                pe.wait_ge(qkx_done, n * 2 + 2)
                for m in range(TT):
                    pe.matmul(bank[m][:], qk_x[:, 0, P * m:P * m + P], qk_x[:, 1, :], start=True, stop=True).then_inc(en_full, 1)
                pe.wait_ge(en_step, n * 5 + 5)
                for k in range(KT):
                    for m in range(TT):
                        mm = pe.transpose(bank[4 + k][:, P * m:P * m + P], e_p[:, m, P * k:P * k + P], ident[:])
                    mm.then_inc(att_full, 1)

            def repack(n):
                for r in range(NB // B):
                    nb = n * (NB // B) + r
                    pe.wait_ge(pk_conv, nb + 1)
                    for half in range(2):
                        use = 2 * r + half
                        if use >= 4:
                            pe.wait_ge((pk_out0, pk_out1)[half], nb - 1)
                        bk = bank[use % 4][:].bitcast(F16)
                        tiles = [[(0, 0), (1, 0)], [(0, 1), (1, 1)], [(2, 0), (3, 0)]] if half == 0 else \
                                [[(2, 1), (3, 1)], [(4, 0), (4, 1)], [(5, 0), (5, 1)]]
                        for q in range(3):
                            for e, (a, w) in enumerate(tiles[q]):
                                mm = pe.transpose(bk[:, 256 * q + P * e:256 * q + P * e + P], pk_16[:, a, P * w:P * w + P], ident16[:])
                        mm.then_inc(pk_full, 1)

            pe.wait_ge(const_done, 3)
            pe.wait_ge(ld_s, 48)
            for i in range(2):
                for q in range(8):
                    if i > 0:
                        pe.wait_ge(st_out, q + 1)
                    for e in range(4):
                        mm = pe.transpose(bank[q][0:16, P * e:P * e + P], gs_in[:, i, 4 * q + e, :], ident[:])
                    mm.then_inc(st_full, 1)
            pe.wait_ge(st_out, 9)
            for t in range(KT):
                mm = pe.transpose(bank[0][:, P * t:P * t + P], ds_in[:, t, :], ident[:])
            mm.then_inc(st_full, 1)
            pe.wait_ge(ld_small, 64)
            pe.wait_ge(st_out, 10)
            for cc in range(2):
                for i in range(2):
                    mm = pe.transpose(bank[1][:, 256 * cc + P * i:256 * cc + P * i + P], xw[:, i, P * cc:P * cc + P], ident[:])
            mm.then_inc(xw_full, 1)
            pe.wait_ge(st_out, 17)
            pe.wait_ge(xw_done, 1)
            pe.wait_ge(ln_done[0], 1)
            spread(0, 0, 0)
            pe.wait_ge(w_lo, 4)
            qkv(0)
            pe.wait_ge(v_out, TT)
            context(0)

            def body(n, last):
                pe.wait_ge(att_lo, n * KT + KT)
                scores(n, 0)
                for u in range(UNITS):
                    if u + 1 < UNITS:
                        scores(n, u + 1)
                    if u > 0:
                        values(n, u - 1)
                    turn(n, u)
                values(n, UNITS - 1)
                if not last:
                    pe.wait_ge(ln_done[0], n + 2)
                    pe.wait_ge(exp_done, (n + 1) * 4 * UNITS)
                    spread(0, n + 1, 0)
                out_proj(n)
                if not last:
                    qkv(n + 1)
                    pe.wait_ge(v_out, (n + 2) * TT)
                pe.wait_ge(ln_done[1], n + 1)
                spread(1, n, 4)
                mix(n)
                if not last:
                    pe.wait_ge(x2_done, n * TT + TT)
                    context(n + 1)
                    pe.wait_ge(en_exp, (n + 2) * TT)
                    pe.wait_ge(att_lo, (n + 2) * KT)
                else:
                    pe.wait_ge(x2_done, n * TT + TT)
                repack(n)
                pe.wait_ge(ln_done[2], n + 1)
                spread(2, n, 4)
                pe.wait_ge(pk_out0, (n + 1) * (NB // B))
                pe.wait_ge(pk_out1, (n + 1) * (NB // B))
                pe.wait_ge(spread_lo[2], (n + 1) * KT)

            walk(body)(pe)

            def gate_up(it, par, s):
                g4 = 4 * ((it // 4) % 2)
                nbl, r = s // 2, s % 2
                if s == 0:
                    pe.wait_ge(in_xf[par], 16 * (it // 2) + 16)
                if s % 2 == 0:
                    pe.wait_ge(dq_lo, 4 * (it // 4) + 2 * nbl + 2)
                for which in range(2):
                    done = (g_full, u_full)[which]
                    bk = bank[2 * (s % 2) + which]
                    if not (isinstance(it, int) and it == 0 and s < 2):
                        pe.wait_ge((sq_out, int_out)[which], 4 * it + s - 1)
                    for k in range(KT):
                        kk, nib = k // 2, k % 2
                        if which == 0:
                            off, at = 0, 256 * kk
                        else:
                            off, at = (0, 512) if kk == 0 else (1, 0)
                        slot = g4 + 2 * nbl + off

                        def w(a):
                            if isinstance(slot, int):
                                return ring[:, a, slot, nib, at + P * r:at + P * r + P]
                            return ring[:, a, bass.ds(slot, 1), nib, at + P * r:at + P * r + P].rearrange("p a c -> p (a c)")
                        mm = three(bk[:], w, lambda a: xf[:, par, a, k, :], k == 0, k == KT - 1)
                    mm.then_inc(done, 1)

            def down(it, par, s):
                g4 = 4 * ((it // 4) % 2)
                nbl, r = s // 2, s % 2
                pe.wait_ge(hid_lo, 4 * it + s + 1)
                if s == 0 and not (isinstance(it, int) and it == 0):
                    pe.wait_ge(acc_out, it)
                slot = g4 + 2 * nbl + 1

                def w(a):
                    if isinstance(slot, int):
                        return ring[:, a, slot, r, 256:768]
                    return ring[:, a, bass.ds(slot, 1), r, 256:768].rearrange("p a c -> p (a c)")
                for t in range(TT):
                    mm = three(bank[4 + t][:], lambda a: hid[:, s % 2, a, P * t:P * t + P], w, s == 0, s == 3)
                mm.then_inc(down_done, 1)

            def iteration(it, par, nxt):
                for s in range(4):
                    if s < 3:
                        gate_up(it, par, s + 1)
                    elif nxt:
                        gate_up(it + 1, 1 - par, 0)
                    down(it, par, s)

            gate_up(0, 0, 0)
            iteration(0, 0, True)
            iteration(1, 1, True)
            with pe.Fori(1, 15) as i2:
                iteration(2 * i2, 0, True)
                iteration(2 * i2 + 1, 1, True)
            iteration(30, 0, True)
            iteration(31, 1, False)

        @block.scalar
        def _(act):
            def spread_heads(st, n, banks):
                for k in range(KT):
                    act.wait_ge(spread_full[st], n * KT + k + 1)
                    nc.scalar.activation(xt[:, 0, k, :], bank[banks + k][:], ACT.Copy, scale=XS).then_inc(spread_hi[st], 1)

            def qkv_heads(n):
                for g in range(12):
                    act.wait_ge(qkv_full, n * 12 + g + 1)
                    if g < 8:
                        if g >= 4:
                            act.wait_ge(stacked[g % 4], n * 512 + 256)
                        elif not isinstance(n, int) or n > 0:
                            act.wait_ge(stacked[g % 4], n * 512)
                        nc.scalar.activation(qk[:, g % 4, 0, :], bank[g % 4][:], ACT.Copy, scale=QS).then_inc(qk_hi, 1)
                    else:
                        nc.scalar.copy(V[:, g - 8, :], bank[g % 4][:]).then_inc(v_out, 1)

            def exp(n, u, j):
                i = u % TT
                act.wait_ge(shift_done, n * 4 * UNITS + 4 * u + j + 1)
                if u >= 2:
                    act.wait_ge(t_full, n * 4 * UNITS + 4 * (u - 2) + j + 1)
                nc.scalar.activation(prob[:, u % 2, j, 0:wide[i]], bank[j][:, 0:wide[i]], ACT.Exp, bias=nmx[:, u % 2, j:j + 1],
                                     scale=C_EXP, accum_out=den[:, u % 2, j:j + 1]).then_inc(exp_done, 1)

            def turned(n, u, j):
                i = u % TT
                act.wait_ge(t_full, n * 4 * UNITS + 4 * u + j + 1)
                if u >= 2:
                    act.wait_ge(av_done, n * UNITS + u - 1)
                nc.scalar.copy(prob_t[:, u % 2, j, 0:wide[i]], bank[4 + j % 2][:, 0:wide[i]]).then_inc(pt_act, 1)

            def out_head(n, hg):
                act.wait_ge(av_done, n * UNITS + 4 * hg + 4)
                nc.scalar.activation(o_t[:, 0, hg, :], bank[6 + hg % 2][:], ACT.Copy, scale=QS).then_inc(o_hi, 1)

            def context(n):
                for cc in range(2):
                    act.wait_ge(ct_full, n * 2 + cc + 1)
                    nc.scalar.copy(c_t[:, cc, :], bank[4 + cc][:]).then_inc(ct_done, 1)
                for i in range(2):
                    act.wait_ge(qkx_full, n * 2 + i + 1)
                    nc.scalar.activation(qk_x[:, i, :], bank[6 + i][:], ACT.Identity, bias=xb[:, i:i + 1]).then_inc(qkx_done, 1)
                for m in range(TT):
                    act.wait_ge(en_max, n * TT + m + 1)
                    nc.scalar.activation(e_p[:, m, :], bank[m][:], ACT.Exp, bias=x_nm[:, m:m + 1],
                                         accum_out=x_den[:, m:m + 1]).then_inc(en_exp, 1)
                for k in range(KT):
                    act.wait_ge(att_full, n * KT + k + 1)
                    nc.scalar.copy(att_t[:, 0, k, :], bank[4 + k][:]).then_inc(att_hi, 1)

            act.wait_ge(fac_step, FAC_STEPS)
            act.wait_ge(ld_w, 64)
            for w in range(4):
                nc.scalar.activation(w_split[:, 0, w], w_raw[:, w], ACT.Copy, scale=fac[:, w:w + 1]).then_inc(w_hi, 1)
            for i in range(2):
                for q in range(8):
                    act.wait_ge(st_full, 8 * i + q + 1)
                    nc.scalar.activation(gu_st[i][:, 512 * q:512 * q + 512], bank[q][0:16, :], ACT.Copy,
                                         scale=(C_SG, C_SU)[i][0:16]).then_inc(st_out, 1)
            act.wait_ge(st_full, 17)
            nc.scalar.activation(d_st[:], bank[0][:], ACT.Copy, scale=C_SD).then_inc(st_out, 1)
            act.wait_ge(xw_full, 1)
            nc.scalar.copy(xw_t[:].rearrange("p a b c -> p (a b c)"), bank[1][:]).then_inc(xw_done, 1)
            spread_heads(0, 0, 0)
            qkv_heads(0)
            act.wait_ge(ld_small, 64)
            act.wait_ge(st_stored, 16 * (4 + NB))
            context(0)

            def body(n, last):
                for j in range(4):
                    if j == 0:
                        act.wait_ge(att_full, n * KT + KT)
                    exp(n, 0, j)
                for u in range(UNITS):
                    for j in range(4):
                        if u + 1 < UNITS:
                            exp(n, u + 1, j)
                        if j > 0:
                            turned(n, u, j - 1)
                    if u > 0 and u % 4 == 0:
                        out_head(n, u // 4 - 1)
                out_head(n, HG - 1)
                if not last:
                    if not isinstance(n, int) or n > 0:
                        act.wait_ge(xf_stored, n * 16)
                    spread_heads(0, n + 1, 0)
                    qkv_heads(n + 1)
                elif B > 1:
                    act.wait_ge(xf_stored, n * 16)
                spread_heads(1, n, 4)
                if not last:
                    context(n + 1)
                for r in range(NB // B):
                    nb = n * (NB // B) + r
                    act.wait_ge(pk_full, 2 * nb + 1)
                    act.wait_ge(pk_stored, 32 * nb)
                    nc.scalar.copy(pk_t[:, 0], bank[2 * r % 4][:].bitcast(F16)[:, 0:HALF]).then_inc(pk_out0, 1)
                spread_heads(2, n, 4)

            walk(body)(act)

            act.wait_ge(xf_stored, 16 * B)
            act.wait_ge(pk_stored, 16 * 2 * NB)

            def dequant(hb, slot):
                act.wait_ge(dq_full, hb + 1)
                nc.scalar.copy(ring[:, 0, slot] if isinstance(slot, int) else ring[:, 0, bass.ds(slot, 1)].rearrange("p a b c -> p (a b) c"),
                               w_full[:]).then_inc(dq_hi, 1)

            def gate(it, s):
                q = s % 2
                step = 4 * it + s
                early = isinstance(it, int) and it == 0 and s < 2
                act.wait_ge(g_full, step + 1)
                if not early:
                    act.wait_ge(gel_out, step - 1)
                nc.scalar.activation(g_sb[:, q], bank[2 * q][:], ACT.Copy, scale=C_G).then_inc(g_out, 1)
                if not early:
                    act.wait_ge(cube_out, step - 1)
                nc.scalar.activation(sq[:, q], bank[2 * q][:], ACT.Square, scale=C_G).then_inc(sq_out, 1)
                act.wait_ge(cube_out, step + 1)
                nc.scalar.activation(th[:, q], cube[:, q], ACT.Tanh, scale=GELU_A * GELU_B).then_inc(th_out, 1)
                act.wait_ge(int_out, step + 1)
                if not early:
                    act.wait_ge(down_done, step - 1)
                nc.scalar.copy(hid[:, q, 0], inter[:, q]).then_inc(hid_hi, 1)

            def iteration(it, deq, nxt):
                for s in range(4):
                    if s < 3:
                        gate(it, s + 1)
                    elif nxt:
                        gate(it + 1, 0)
                    if s == 0 and deq:
                        if not isinstance(it, int) or it >= 4:
                            act.wait_ge(down_done, 4 * (it // 4) * 4)
                        dequant(it + 4, (it + 4) % 8)

            for hb in range(4):
                dequant(hb, hb)
            gate(0, 0)
            iteration(0, True, True)
            with act.Fori(1, 28) as it:
                iteration(it, True, True)
            with act.Fori(28, 31) as it:
                iteration(it, False, True)
            iteration(31, False, False)

        @block.vector
        def _(dve):
            def norm(st, n):
                steps = Steps(dve, ln_step[st], n * LN_STEPS, LN_STEPS)
                tile = lambda t: X[:, t, :] if isinstance(t, int) else X[:, bass.ds(t, 1), :].rearrange("p a d -> p (a d)")
                for t in range(TT):
                    steps.mark(nc.vector.bn_stats(st6[:, t, :], tile(n * TT + t)))
                alone(dve, steps.sem, steps.base + steps.k)
                for t in range(TT):
                    steps.mark(nc.vector.bn_aggr(mv[:, t, :], st6[:, t, :]))
                steps.settle()
                steps.mark(nc.vector.tensor_scalar(var[:], mv[:, :, 1], EPS, None, ALU.add))
                steps.settle()
                steps.mark(nc.vector.tensor_scalar(rsi[:], var[:].bitcast(I32), 1, None, ALU.logical_shift_right))
                steps.settle()
                steps.mark(nc.vector.tensor_scalar(rs[:, 0].bitcast(I32), rsi[:], -1.0, float(0x5F3759DF), ALU.mult, ALU.add))
                for _ in range(3):
                    steps.settle()
                    steps.mark(nc.vector.tensor_tensor(rs[:, 1], rs[:, 0], rs[:, 0], ALU.mult))
                    steps.settle()
                    steps.mark(nc.vector.scalar_tensor_tensor(rs[:, 1], rs[:, 1], -0.5, var[:], ALU.mult, ALU.mult))
                    steps.settle()
                    steps.mark(nc.vector.scalar_tensor_tensor(rs[:, 0], rs[:, 1], 1.5, rs[:, 0], ALU.add, ALU.mult))
                steps.settle()
                for t in range(TT):
                    ins = nc.vector.tensor_scalar(xn[:, t, :], tile(n * TT + t), mv[:, t, 0:1], rs[:, 0, t:t + 1], ALU.subtract, ALU.mult)
                ins.then_inc(ln_done[st], 1)
                steps.end()

            def spread_tails(st, n, banks):
                for k in range(KT):
                    dve.wait_ge(spread_hi[st], n * KT + k + 1)
                    nc.vector.scalar_tensor_tensor(xt[:, 1, k, :], bank[banks + k][:], XS, xt[:, 0, k, :],
                                                   ALU.mult, ALU.subtract).then_inc(spread_lo[st], 1)

            def qkv_tails(n):
                for g in range(8):
                    dve.wait_ge(qk_hi, n * 8 + g + 1)
                    nc.vector.scalar_tensor_tensor(qk[:, g % 4, 1, :], bank[g % 4][:], QS, qk[:, g % 4, 0, :],
                                                   ALU.mult, ALU.subtract).then_inc(qk_lo, 1)

            def row_max(n, u, j):
                i = u % TT
                alone(dve, s_full, n * 4 * UNITS + 4 * u + j + 1)
                nc.vector.tensor_tensor_reduce(out=bank[j][:, 0:wide[i]], in0=bank[j][:, 0:wide[i]],
                                               in1=mask[:, P * (3 - i):P * (3 - i) + wide[i]], scale=1.0,
                                               scalar=0.0 if i < TT - 1 else NEG, op0=ALU.mult, op1=ALU.max,
                                               accum_out=mx[:, u % 2, j:j + 1]).then_inc(max_done, 1)

            def shift(n, u, j):
                dve.wait_ge(max_done, n * 4 * UNITS + 4 * u + j + 1)
                nc.vector.tensor_scalar(nmx[:, u % 2, j:j + 1], mx[:, u % 2, j:j + 1], C_NEXP, None, ALU.mult).then_inc(shift_done, 1)

            def recip(n, u):
                i = u % TT
                base = n * UNIT_DEN[UNITS] + UNIT_DEN[u]
                dve.wait_ge(exp_done, n * 4 * UNITS + 4 * u + 4)
                beyond = T - wide[i]
                if DEN_STEPS[i] == 2:
                    nc.vector.scalar_tensor_tensor(den[:, u % 2, :], prob[:, u % 2, :, wide[i] - 1], float(beyond), den[:, u % 2, :],
                                                   ALU.mult, ALU.add).then_inc(den_step, 1)
                    dve.wait_ge(den_step, base + 1)
                nc.vector.reciprocal(rden[:, u % 2, :], den[:, u % 2, :]).then_inc(den_step, 1)
                dve.wait_ge(den_step, base + DEN_STEPS[i])

            def normalise(n, u, j):
                w = wide[u % TT]
                nc.vector.tensor_scalar(prob[:, u % 2, j, 0:w], prob[:, u % 2, j, 0:w], rden[:, u % 2, j:j + 1], None,
                                        ALU.mult).then_inc(norm_done, 1)

            def turned(n, u):
                i = u % TT
                dve.wait_ge(t_full, n * 4 * UNITS + 4 * u + 4)
                if u >= 2:
                    dve.wait_ge(av_done, n * UNITS + u - 1)
                nc.vector.tensor_copy(prob_t[:, u % 2, 3, 0:wide[i]], bank[5][:, 0:wide[i]]).then_inc(pt_dve, 1)

            def out_tail(n, hg):
                dve.wait_ge(o_hi, n * HG + hg + 1)
                nc.vector.scalar_tensor_tensor(o_t[:, 1, hg, :], bank[6 + hg % 2][:], QS, o_t[:, 0, hg, :],
                                               ALU.mult, ALU.subtract).then_inc(o_lo, 1)

            def residual(n, full, banks, factor, done):
                for t in range(TT):
                    dve.wait_ge(full, n * TT + t + 1)
                    at = n * TT + t
                    xv = X[:, at, :] if isinstance(at, int) else X[:, bass.ds(at, 1), :].rearrange("p a d -> p (a d)")
                    nc.vector.scalar_tensor_tensor(xv, bank[banks + t][:], factor, xv, ALU.mult, ALU.add).then_inc(done, 1)
                alone(dve, done, n * TT + TT)

            def context(n):
                for m in range(TT):
                    dve.wait_ge(en_full, n * TT + m + 1)
                    nc.vector.tensor_reduce(x_nm[:, m:m + 1], bank[m][:], AX.X, ALU.max, negate=True).then_inc(en_max, 1)
                dve.wait_ge(en_exp, n * TT + TT)
                nc.vector.reciprocal(x_rden[:], x_den[:]).then_inc(en_step, 1)
                dve.wait_ge(en_step, n * 5 + 1)
                for m in range(TT):
                    nc.vector.tensor_scalar(e_p[:, m, :], e_p[:, m, :], x_rden[:, m:m + 1], AS, ALU.mult, ALU.mult).then_inc(en_step, 1)

            def context_tails(n):
                for k in range(KT):
                    dve.wait_ge(att_hi, n * KT + k + 1)
                    nc.vector.tensor_tensor(att_t[:, 1, k, :], bank[4 + k][:], att_t[:, 0, k, :], ALU.subtract).then_inc(att_lo, 1)

            dve.wait_ge(ld_w, 64)
            for w in range(4):
                nc.vector.tensor_reduce(most[:, w:w + 1], w_raw[:, w].rearrange("p k n -> p (k n)"), AX.X, ALU.max,
                                        apply_absolute_value=True).then_inc(most_done, 1)
            dve.wait_ge(ld_s, 48)
            for i in range(2):
                nc.vector.tensor_reduce(most[:, SG + i:SG + i + 1], gs_in[:, i].rearrange("p n k -> p (n k)"), AX.X, ALU.max,
                                        apply_absolute_value=True).then_inc(most_done, 1)
            nc.vector.tensor_reduce(most[:, SD:SD + 1], ds_in[:].rearrange("p t k -> p (t k)"), AX.X, ALU.max,
                                    apply_absolute_value=True).then_inc(most_done, 1)
            dve.wait_ge(ld_x0, 16)
            norm(0, 0)
            dve.wait_ge(all_done, 1)
            steps = Steps(dve, fac_step, 0, FAC_STEPS)
            e0, e1 = expo[:, 0], expo[:, 1]
            steps.mark(nc.vector.tensor_scalar(e0, most_all[:].bitcast(I32), 23, None, ALU.logical_shift_right))
            steps.settle()
            steps.mark(nc.vector.tensor_scalar(e1, e0, -1.0, float(TOP + 127), ALU.mult, ALU.add))
            steps.settle()
            steps.mark(nc.vector.tensor_scalar(e0, e1, float(CAP), None, ALU.min))
            steps.settle()
            steps.mark(nc.vector.tensor_scalar(fac[:].bitcast(I32), e0, 23, None, ALU.logical_shift_left))
            steps.mark(nc.vector.tensor_scalar(e1, e0, -1.0, 254.0, ALU.mult, ALU.add))
            steps.settle()
            steps.mark(nc.vector.tensor_scalar(ifac[:].bitcast(I32), e1, 23, None, ALU.logical_shift_left))
            steps.settle()

            def pair(dst, a, s, b):
                steps.mark(nc.vector.scalar_tensor_tensor(dst, a, s, b, ALU.mult, ALU.mult))

            def one(dst, a, s):
                steps.mark(nc.vector.tensor_scalar(dst, a, s, None, ALU.mult))

            f = lambda i: fac[:, i:i + 1]
            r = lambda i: ifac[:, i:i + 1]
            pair(C_EXP, r(0), 2.0 ** 14 / float(np.sqrt(T)), r(1))
            pair(C_NEXP, r(0), -(2.0 ** 14) / float(np.sqrt(T)), r(1))
            pair(C_O, r(2), 2.0 ** 7, r(3))
            one(C_G, r(SG), 1.0 / XS)
            one(C_I, f(SG), 2.0 ** -46)
            pair(tmpc[:, 0:1], r(SG), 2.0 ** 34, r(SU))
            one(C_SG, f(SG), LUT)
            one(C_SU, f(SU), LUT)
            one(C_SD, f(SD), LUT)
            steps.settle()
            steps.mark(nc.vector.tensor_tensor(C_OUT, tmpc[:, 0:1], r(SD), ALU.mult))
            steps.settle()
            steps.end()
            for w in range(4):
                dve.wait_ge(w_hi, w + 1)
                nc.vector.scalar_tensor_tensor(w_split[:, 1, w], w_raw[:, w], fac[:, w:w + 1], w_split[:, 0, w],
                                               ALU.mult, ALU.subtract).then_inc(w_lo, 1)
            spread_tails(0, 0, 0)
            dve.wait_ge(w_lo, 4)
            qkv_tails(0)
            context(0)
            context_tails(0)
            dve.wait_ge(const_done, 3)
            dve.wait_ge(ld_x, 16 * (B - 1))

            def body(n, last):
                if not last:
                    norm(0, n + 1)
                for j in range(4):
                    row_max(n, 0, j)
                    if j > 0:
                        shift(n, 0, j - 1)
                shift(n, 0, 3)
                for u in range(UNITS):
                    nxt = u + 1 < UNITS
                    if u > 0:
                        turned(n, u - 1)
                    if nxt:
                        row_max(n, u + 1, 0)
                        row_max(n, u + 1, 1)
                        shift(n, u + 1, 0)
                    recip(n, u)
                    normalise(n, u, 0)
                    normalise(n, u, 1)
                    if nxt:
                        row_max(n, u + 1, 2)
                        shift(n, u + 1, 1)
                    normalise(n, u, 2)
                    if nxt:
                        row_max(n, u + 1, 3)
                        shift(n, u + 1, 2)
                    normalise(n, u, 3)
                    if nxt:
                        shift(n, u + 1, 3)
                    if u > 0 and u % 4 == 0:
                        out_tail(n, u // 4 - 1)
                turned(n, UNITS - 1)
                out_tail(n, HG - 1)
                if not last:
                    spread_tails(0, n + 1, 0)
                residual(n, wo_full, 4, C_O, x1_done)
                norm(1, n)
                if not last:
                    qkv_tails(n + 1)
                spread_tails(1, n, 4)
                residual(n, mix_full, 0, 1.0 / (XS * AS), x2_done)
                norm(2, n)
                if not last:
                    context(n + 1)
                    context_tails(n + 1)
                for r in range(NB // B):
                    nb = n * (NB // B) + r
                    dve.wait_ge(pk_full, 2 * nb + 2)
                    dve.wait_ge(pk_stored, 32 * nb)
                    nc.vector.tensor_copy(pk_t[:, 1], bank[(2 * r + 1) % 4][:].bitcast(F16)[:, 0:HALF]).then_inc(pk_out1, 1)
                spread_tails(2, n, 4)

            walk(body)(dve)

            dve.wait_ge(xf_stored, 16 * B)
            dve.wait_ge(pk_stored, 16 * 2 * NB)

            def dequant(hb, slot, par):
                steps = Steps(dve, dq_step, hb * 6, 6)
                dve.wait_ge(in_pk[par], 32 * (hb // 2) + 32)
                words = pk_in2[:, par].bitcast(U32)
                for nib in range(2):
                    steps.mark(nc.vector.tensor_scalar(bits[:, nib], words, 9 - 4 * nib, 0x0E000E00,
                                                       ALU.logical_shift_left, ALU.bitwise_and))
                    steps.mark(nc.vector.tensor_scalar(codes[:, nib], words, 12 - 4 * nib, 0x80008000,
                                                       ALU.logical_shift_left, ALU.bitwise_and))
                steps.settle()
                for nib in range(2):
                    steps.mark(nc.vector.tensor_tensor(codes[:, nib], codes[:, nib], bits[:, nib], ALU.bitwise_or))
                steps.settle()
                steps.end()
                if not isinstance(hb, int) or hb > 0:
                    dve.wait_ge(dq_lo, hb)
                sc = sc_in[:, par]
                nc.vector.tensor_tensor(w_full[:], codes[:].rearrange("p a c -> p (a c)").bitcast(F16).rearrange("p (a c) -> p a c", a=2),
                                        sc.unsqueeze(1).to_broadcast([P, 2, HALF]), ALU.mult).then_inc(dq_full, 1)
                dve.wait_ge(dq_hi, hb + 1)
                lo, hi = (ring[:, a, slot] if isinstance(slot, int) else ring[:, a, bass.ds(slot, 1)].rearrange("p a b c -> p (a b) c") for a in (1, 0))
                nc.vector.tensor_tensor(lo, w_full[:], hi, ALU.subtract).then_inc(dq_lo, 1)

            def gate(it, s):
                q = s % 2
                step = 4 * it + s
                early = isinstance(it, int) and it == 0 and s < 2
                dve.wait_ge(sq_out, step + 1)
                if not early:
                    dve.wait_ge(th_out, step - 1)
                nc.vector.scalar_tensor_tensor(cube[:, q], sq[:, q], 1.0 / GELU_B, g_sb[:, q], ALU.add, ALU.mult).then_inc(cube_out, 1)
                dve.wait_ge(th_out, step + 1)
                nc.vector.scalar_tensor_tensor(gel[:, q], th[:, q], 1.0, g_sb[:, q], ALU.add, ALU.mult).then_inc(gel_out, 1)
                dve.wait_ge(gel_out, step + 1)
                dve.wait_ge(u_full, step + 1)
                nc.vector.scalar_tensor_tensor(inter[:, q], bank[2 * q + 1][:], C_I, gel[:, q], ALU.mult, ALU.mult).then_inc(int_out, 1)
                dve.wait_ge(hid_hi, step + 1)
                nc.vector.tensor_tensor(hid[:, q, 1], inter[:, q], hid[:, q, 0], ALU.subtract).then_inc(hid_lo, 1)

            def add_out(it):
                dve.wait_ge(down_done, 4 * it + 4)
                for t in range(TT):
                    at = (it % B) * TT + t
                    xv = X[:, at, :] if isinstance(at, int) else X[:, bass.ds(at, 1), :].rearrange("p a d -> p (a d)")
                    ins = nc.vector.scalar_tensor_tensor(xv, bank[4 + t][:], C_OUT, xv, ALU.mult, ALU.add)
                ins.then_inc(acc_out, 1)

            def iteration(it, par, deq, nxt):
                for s in range(4):
                    if s < 3:
                        gate(it, s + 1)
                    elif nxt:
                        gate(it + 1, 0)
                    if s == 0 and deq:
                        dequant(it + 4, (it + 4) % 8, par)
                add_out(it)

            for hb in range(4):
                dequant(hb, hb, hb % 2)
            gate(0, 0)
            iteration(0, 0, True, True)
            iteration(1, 1, True, True)
            with dve.Fori(1, 14) as i2:
                iteration(2 * i2, 0, True, True)
                iteration(2 * i2 + 1, 1, True, True)
            with dve.Fori(28, 31) as it:
                iteration(it, 0, False, True)
            iteration(31, 1, False, False)


FAC_STEPS = 6 + 10
GELU_A = 0.7978845608028654
GELU_B = 0.044715

_INS = ["x", "ctx_1024", "L0_attn_Wq", "L0_attn_Wk", "L0_attn_Wv", "L0_attn_Wo", "L0_xattn_Wq", "L0_xattn_bq",
        "L0_xattn_Wk", "L0_xattn_bk", "L0_ffn_gate_W_packed", "L0_ffn_gate_scales", "L0_ffn_up_W_packed",
        "L0_ffn_up_scales", "L0_ffn_down_W_packed", "L0_ffn_down_scales"]
_OUTS = [((4, 512, 512), "float32")]


def kernel(**inputs):
    import numpy as _np
    import concourse.bacc as _bacc
    from concourse import mybir as _mybir
    from concourse.bass_utils import run_bass_kernel_spmd as _run

    nc = _bacc.Bacc("TRN2", target_bir_lowering=False, num_devices=1)
    arrays, args = {}, []
    for name in _INS:
        a = _np.ascontiguousarray(inputs[name])
        arrays[f"in_{name}_dram"] = a
        args.append(nc.dram_tensor(f"in_{name}_dram", a.shape, _mybir.dt.from_np(a.dtype), kind="ExternalInput").ap())
    for i, (shape, dtype) in enumerate(_OUTS):
        dt = _mybir.dt.from_np(_np.dtype(dtype))
        args.append(nc.dram_tensor(f"out_{i}_dram", shape, dt, kind="ExternalOutput").ap())
    decoder_layer(nc, *args)
    r = _run(nc, [arrays], core_ids=[0])
    got = tuple(r.results[0][f"out_{i}_dram"] for i in range(len(_OUTS)))
    return got[0]
```

```python
from contextlib import ExitStack

import numpy as np

import concourse.bass as bass
from concourse import mybir

F32 = mybir.dt.float32
F16 = mybir.dt.float16
I32 = mybir.dt.int32
U32 = mybir.dt.uint32
I16 = mybir.dt.int16
U8 = mybir.dt.uint8
ALU = mybir.AluOpType
ACT = mybir.ActivationFunctionType
AX = mybir.AxisListType
RMAX = bass.bass_isa.ReduceOp.max

P = 128
B, T, D = 4, 512, 512
HEADS, DH = 16, 32
C, DX = 256, 128
F = 4096
QBLOCK = 32
TT = T // P
KT = D // P
HG = HEADS // 4
UNITS = HG * TT
NB = F // 256
HALF = 768
EPS = 1e-5

XS = 2.0 ** 11
QS = 2.0 ** -18
AS = 2.0 ** 14
TOP = 127 + 12
CAP = 127 + 60
LUT = 2.0 ** 14
NEG = -3.0e38

WEIGHTS = ("q", "k", "v", "o")
SG, SU, SD = 4, 5, 6


class Steps:

    def __init__(self, eng, sem, base, per):
        self.eng, self.sem, self.base, self.per, self.k = eng, sem, base, per, 0

    def mark(self, ins):
        ins.then_inc(self.sem, 1)
        self.k += 1

    def settle(self):
        self.eng.wait_ge(self.sem, self.base + self.k)

    def end(self):
        assert self.k == self.per, (self.k, self.per)


def decoder_layer(nc, x, ctx_1024, Wq, Wk, Wv, Wo, xWq, xbq, xWk, xbk, gate_p, gate_s, up_p, up_s, down_p, down_s, out):
    with ExitStack() as ctx:
        def sem(name):
            return ctx.enter_context(nc.semaphore(name))

        def psum(name, shape, dt):
            return ctx.enter_context(nc.psum_tensor(name, shape, dt))

        def keep(name, shape, dt):
            return ctx.enter_context(nc.sbuf_tensor(name, shape, dt))

        packed_t = nc.dram_tensor("packed_t", (2 * NB, P, HALF), I16, kind="Internal").ap()
        scale_t = nc.dram_tensor("scale_t", (2 * NB, 8, HALF), F32, kind="Internal").ap()
        qk_dram = nc.dram_tensor("qk_dram", (2, 2, D, T), F16, kind="Internal").ap()
        xf_dram = nc.dram_tensor("xf_dram", (B, P, 2 * KT * T), F16, kind="Internal").ap()

        bank = [psum(f"bank{i}", [P, 512], F32) for i in range(8)]
        X = keep("X", [P, B * TT, D], F32)
        fac = keep("fac", [P, 7], F32)
        ifac = keep("ifac", [P, 7], F32)
        col = keep("col", [P, 12], F32)
        C_EXP, C_NEXP, C_O, C_G, C_I, C_OUT, C_SG, C_SU, C_SD = (col[:, i:i + 1] for i in range(9))
        tmpc = keep("tmpc", [P, 4], F32)

        first = ExitStack()

        def sb(name, shape, dt):
            return first.enter_context(nc.sbuf_tensor(name, shape, dt))

        stack = sb("stack", [P, 2, HEADS, T], F16)
        w_raw = stack[:].rearrange("p a h t -> p (a h t)").bitcast(F32).rearrange("p (w k n) -> p w k n", w=4, k=KT)
        w_split = sb("w_split", [P, 2, 4, KT, D], F16)
        xn = sb("xn", [P, TT, D], F32)
        xt = sb("xt", [P, 2, KT, T], F16)
        qk = sb("qk", [P, 4, 2, T], F16)
        V = sb("V", [P, TT, D], F32)
        v_tail = sb("v_tail", [P, 2, D], F32)
        prob = sb("prob", [P, 2, 4, T], F32)
        prob_t = sb("prob_t", [P, 2, 4, T], F32)
        o_t = sb("o_t", [P, 2, HG, T], F16)
        att_t = sb("att_t", [P, 2, KT, T], F16)
        c_in = sb("c_in", [P, TT, C], F32)
        c_t = prob_t[:, 0, 0:2, :]
        qk_x = prob_t[:, 1, 0:2, :]
        e_p = prob[:, 0, :, :]
        xw = sb("xw", [P, 2, C], F32)
        xw_t = sb("xw_t", [P, 2, 2, DX], F32)
        xb = sb("xb", [P, 2], F32)
        o_sum = sb("o_sum", [P, T], F32)
        r_den = sb("r_den", [P, 2, P], F32)
        counts = sb("counts", [P, 3, 32], F32)
        mask = sb("mask", [P, 5 * P], F32)
        ident = sb("ident", [P, P], F32)
        ident16 = sb("ident16", [P, P], F16)
        ones = V[:].rearrange("p t d -> p (t d)")[:, 0:5 * P]
        o_raw = o_t[:].rearrange("p a h t -> p (a h t)").bitcast(F32)
        gs_in = o_raw[:, 0:1024].rearrange("p (i n k) -> p i n k", i=2, k=D // QBLOCK)
        ds_in = o_raw[:, 1024:1536].rearrange("p (t k) -> p t k", t=KT)
        gu_st = [prob[0:16].rearrange("p a j t -> p (a j t)"), prob_t[0:16].rearrange("p a j t -> p (a j t)")]
        d_st = v_tail[:, 0]
        most = sb("most", [P, 7], F32)
        most_all = sb("most_all", [P, 7], F32)
        expo = sb("expo", [P, 2, 7], I32)
        pk_in = sb("pk_in", [P, 6, C], I32)
        pk_16 = sb("pk_16", [P, 6, C], F16)
        pk_t = sb("pk_t", [P, 2, HALF], I16)
        st6 = sb("st6", [P, TT, 6], F32)
        mv = sb("mv", [P, TT, 2], F32)
        var = sb("var", [P, TT], F32)
        rs = sb("rs", [P, 2, TT], F32)
        rsi = sb("rsi", [P, TT], I32)
        mx = sb("mx", [P, 2, 4], F32)
        nmx = sb("nmx", [P, 2, 4], F32)
        x_nm = sb("x_nm", [P, 4], F32)
        x_den = sb("x_den", [P, 4], F32)
        x_rden = sb("x_rden", [P, 4], F32)
        first.close()

        second = ExitStack()

        def sb2(name, shape, dt):
            return second.enter_context(nc.sbuf_tensor(name, shape, dt))

        ring = sb2("ring", [P, 2, 8, 2, HALF], F16)
        xf = sb2("xf", [P, 2, 2, KT, T], F16)
        pk_in2 = sb2("pk_in2", [P, 2, HALF], I16)
        sc_in = sb2("sc_in", [P, 2, HALF], F32)
        bits = sb2("bits", [P, 2, HALF // 2], U32)
        codes = sb2("codes", [P, 2, HALF // 2], U32)
        w_full = sb2("w_full", [P, 2, HALF], F32)
        g_sb = sb2("g_sb", [P, 2, T], F32)
        sq = sb2("sq", [P, 2, T], F32)
        cube = sb2("cube", [P, 2, T], F32)
        th = sb2("th", [P, 2, T], F32)
        gel = sb2("gel", [P, 2, T], F32)
        inter = sb2("inter", [P, 2, T], F32)
        hid = sb2("hid", [P, 2, 2, T], F16)
        second.close()

        ld_w, ld_s, ld_x0, ld_x, ld_small = (sem(n) for n in ("ld_w", "ld_s", "ld_x0", "ld_x", "ld_small"))
        ld_ctx, ld_pk = sem("ld_ctx"), sem("ld_pk")
        const_ones, const_done = sem("const_ones"), sem("const_done")
        most_done, all_done, fac_step = sem("most_done"), sem("all_done"), sem("fac_step")
        w_hi, w_lo = sem("w_hi"), sem("w_lo")
        st_full, st_out, st_stored = sem("st_full"), sem("st_out"), sem("st_stored")
        xw_full, xw_done = sem("xw_full"), sem("xw_done")
        ln_step = [sem(f"ln{i}_step") for i in range(3)]
        ln_done = [sem(f"ln{i}_done") for i in range(3)]
        spread_full = [sem(f"spread{i}_full") for i in range(3)]
        spread_hi = [sem(f"spread{i}_hi") for i in range(3)]
        spread_lo = [sem(f"spread{i}_lo") for i in range(3)]
        qkv_full, qk_hi, qk_lo, v_out, vt_step = (sem(n) for n in ("qkv_full", "qk_hi", "qk_lo", "v_out", "vt_step"))
        stacked = [sem(f"stacked{i}") for i in range(4)]
        s_full, max_done, shift_done, exp_done = (sem(n) for n in ("s_full", "max_done", "shift_done", "exp_done"))
        qk_in, t_full = [sem(f"qk_in{i}") for i in range(4)], sem("t_full")
        pt_act, pt_dve, av_done, o_step, o_hi, o_lo = (sem(n) for n in ("pt_act", "pt_dve", "av_done", "o_step", "o_hi", "o_lo"))
        wo_full, x1_done, mix_full, x2_done = (sem(n) for n in ("wo_full", "x1_done", "mix_full", "x2_done"))
        ct_full, ct_done, qkx_full, qkx_done = (sem(n) for n in ("ct_full", "ct_done", "qkx_full", "qkx_done"))
        en_full, en_max, en_exp, en_step, att_full, att_hi, att_lo = (
            sem(n) for n in ("en_full", "en_max", "en_exp", "en_step", "att_full", "att_hi", "att_lo"))
        pk_conv, pk_full, pk_out0, pk_out1, pk_stored = (sem(n) for n in ("pk_conv", "pk_full", "pk_out0", "pk_out1", "pk_stored"))
        xf_stored = sem("xf_stored")
        in_pk, in_xf = [sem("in_pk0"), sem("in_pk1")], [sem("in_xf0"), sem("in_xf1")]
        dq_step, dq_full, dq_hi, dq_lo = (sem(n) for n in ("dq_step", "dq_full", "dq_hi", "dq_lo"))
        g_full, u_full, g_out, sq_out, cube_out, th_out = (sem(n) for n in ("g_full", "u_full", "g_out", "sq_out", "cube_out", "th_out"))
        gel_out, int_out, hid_hi, hid_lo, down_done, acc_full, acc_out = (
            sem(n) for n in ("gel_out", "int_out", "hid_hi", "hid_lo", "down_done", "acc_full", "acc_out"))
        out_stored, passed = sem("out_stored"), sem("passed")

        LN_STEPS = 4 + 4 + 3 + 9
        ROWS = 4 * UNITS
        wide = [min(T, (i + 2) * P) for i in range(TT)]

        def alone(eng, sem, value):
            eng.wait_ge(sem, value)
            eng.sem_inc(passed, 1)

        def walk(body):
            def run(eng):
                with eng.Fori(0, B - 1) as n:
                    body(n, False)
                body(B - 1, True)
            return run

        block = ctx.enter_context(nc.Block())

        @block.sync
        def _(sp):
            sp.sem_inc(xf_stored, 16)
            sp.dma_start(X[:, 0:TT, :], x[0].rearrange("(t p) d -> p t d", p=P)).then_inc(ld_x0, 16)
            for w, src in enumerate((Wq, Wk, Wv, Wo)):
                sp.dma_start(w_raw[:, w], src.rearrange("(k p) n -> p k n", p=P)).then_inc(ld_w, 16)
            for i, src in enumerate((gate_s, up_s)):
                sp.dma_start(gs_in[:, i].rearrange("p (n r) k -> p n (r k)", r=2),
                             src.rearrange("(n p r) k -> p n (r k)", p=P, r=2)).then_inc(ld_s, 16)
            sp.dma_start(ds_in[:], down_s.rearrange("(t p) k -> p t k", p=P)).then_inc(ld_s, 16)
            for i, (w, bv) in enumerate(((xWq, xbq), (xWk, xbk))):
                sp.dma_start(xw[:, i], w).then_inc(ld_small, 16)
                sp.dma_start(xb[:, i:i + 1], bv.rearrange("(p a) -> p a", a=1)).then_inc(ld_small, 16)
            for b in range(1, B):
                sp.dma_start(X[:, b * TT:(b + 1) * TT, :], x[b].rearrange("(t p) d -> p t d", p=P)).then_inc(ld_x, 16)

            def load_ctx(n):
                if not isinstance(n, int) or n > 0:
                    sp.wait_ge(ct_full, n * 2)
                sp.dma_start(c_in[:], ctx_1024[n].rearrange("(t p) c -> p t c", p=P) if isinstance(n, int)
                             else ctx_1024[bass.ds(n, 1)].rearrange("a (t p) c -> p (a t) c", p=P)).then_inc(ld_ctx, 16)

            def stack_heads(n):
                def fetch(g):
                    c, which = g // 2, g % 2
                    sp.wait_ge(qk_in[g % 4], n * 32 + 16 * (g // 4) + 16)
                    for part in range(4):
                        hl = part % 2 if which == 0 else part // 2
                        sp.dma_start(stack[32 * part:32 * part + 32, which, 4 * c:4 * c + 4, :],
                                     qk_dram[which, hl, P * c:P * c + P, :].rearrange("(j d) t -> d j t", d=DH)).then_inc(stacked[g % 4], 16)

                for g in range(2 * HG):
                    c, which = g // 2, g % 2
                    sp.wait_ge(qk_lo, n * 2 * HG + g + 1)
                    sp.dma_start(qk_dram[which, :, P * c:P * c + P, :].rearrange("a p t -> p a t"), qk[:, g % 4]).then_inc(qk_in[g % 4], 16)
                    if g > 0:
                        fetch(g - 1)
                fetch(2 * HG - 1)

            load_ctx(0)
            for i in range(2):
                sp.wait_ge(st_out, 8 * (i + 1))
                for kk in range(2):
                    hb, piece = (0, kk) if i == 0 else (kk, 2 * (1 - kk))
                    dst = scale_t.rearrange("(n a) k c -> k n a c", a=2)[:, :, hb, 256 * piece:256 * piece + 256]
                    sp.dma_start(dst, gu_st[i][8 * kk:8 * kk + 8, :].rearrange("k (n c) -> k n c", n=NB)).then_inc(st_stored, 16)
            sp.wait_ge(st_out, 17)
            for nb in range(NB):
                sp.dma_start(scale_t[2 * nb + 1, :, 256:768], d_st[8 * nb:8 * nb + 8, :]).then_inc(st_stored, 16)
            stack_heads(0)

            def load_packed(nb):
                for i, src in enumerate((gate_p, up_p)):
                    rows = src.rearrange("(n p r) w -> n p r w", p=P, r=2)
                    sp.dma_start(pk_in[:, 2 * i:2 * i + 2, :], rows[bass.ds(nb, 1)].rearrange("a p r w -> p (a r) w")).then_inc(ld_pk, 16)
                cols = down_p.rearrange("(t p) (n w) -> n p t w", p=P, w=P)
                sp.dma_start(pk_in[:, 4:6, :].rearrange("p a (b w) -> p (a b) w", w=P),
                             cols[bass.ds(nb, 1)].rearrange("a p t w -> p (a t) w")).then_inc(ld_pk, 16)

            def body(n, last):
                first_nb = n * (NB // B)
                load_packed(first_nb)
                for r in range(NB // B):
                    nb = first_nb + r
                    if r + 1 < NB // B:
                        sp.wait_ge(pk_conv, nb + 1)
                        load_packed(nb + 1)
                    sp.wait_ge(pk_out0, nb + 1)
                    sp.dma_start(packed_t[bass.ds(2 * nb, 1)].rearrange("a p c -> p (a c)"), pk_t[:, 0]).then_inc(pk_stored, 16)
                    sp.wait_ge(pk_out1, nb + 1)
                    sp.dma_start(packed_t[bass.ds(2 * nb + 1, 1)].rearrange("a p c -> p (a c)"), pk_t[:, 1]).then_inc(pk_stored, 16)
                sp.wait_ge(pk_stored, 32 * (first_nb + NB // B))
                if not last:
                    load_ctx(n + 1)
                    stack_heads(n + 1)
                sp.wait_ge(spread_lo[2], (n + 1) * KT)
                sp.dma_start(xf_dram[bass.ds(n, 1)].rearrange("a p c -> p (a c)"),
                             xt[:].rearrange("p a k t -> p (a k t)")).then_inc(xf_stored, 16)

            walk(body)(sp)

            sp.wait_ge(xf_stored, 16 * B + 16)
            sp.wait_ge(pk_stored, 16 * 2 * NB)
            sp.wait_ge(st_stored, 16 * (4 + NB))

            def load_half(hb, slot, ready):
                sp.dma_start(pk_in2[:, slot], packed_t[bass.ds(hb, 1)].rearrange("a p c -> p (a c)")).then_inc(in_pk[ready], 16)
                rows = scale_t[bass.ds(hb, 1)]
                sp.dma_start(sc_in[:, slot], bass.AP(rows.tensor, rows.offset, [[HALF, 8], [0, 16], [1, HALF]])).then_inc(in_pk[ready], 16)

            def load_xf(b, slot, ready):
                sp.dma_start(xf[:, slot].rearrange("p a k t -> p (a k t)"),
                             xf_dram[bass.ds(b, 1)].rearrange("a p c -> p (a c)")).then_inc(in_xf[ready], 16)

            load_xf(0, 0, 0)
            for hb in range(4):
                if hb >= 2:
                    sp.wait_ge(dq_full, hb - 1)
                load_half(hb, hb % 2, hb % 2)

            def mlp_loads(i2, odd, dequant, nxt):
                it = 2 * i2 + odd
                if dequant:
                    sp.wait_ge(dq_full, it + 3)
                    load_half(it + 4, odd, odd)
                if nxt:
                    if not isinstance(it, int) or it > 0:
                        sp.wait_ge(down_done, 4 * it - 1 + 1)
                    load_xf((it + 1) % B, 1 - odd, 1 - odd)

            def store(it):
                sp.wait_ge(acc_out, it + 1)
                sp.dma_start(out[it % B].rearrange("(t p) d -> p t d", p=P), X[:, (it % B) * TT:(it % B + 1) * TT, :]).then_inc(out_stored, 16)

            mlp_loads(0, 0, True, True)
            mlp_loads(0, 1, True, True)
            with sp.Fori(1, 14) as i2:
                mlp_loads(i2, 0, True, True)
                mlp_loads(i2, 1, True, True)
            for it in range(28, 32):
                mlp_loads(it // 2, it % 2, False, it < 31)
                if it > 28:
                    store(it - 1)
            store(31)
            sp.wait_ge(out_stored, 16 * B)

        @block.gpsimd
        def _(pool):
            nc.gpsimd.memset(ones[:], 1.0).then_inc(const_ones, 1)
            pool.wait_ge(const_ones, 1)
            nc.gpsimd.affine_select(out=mask[:], in_=ones[:], compare_op=ALU.is_ge, fill=0.0, base=3 * P,
                                    pattern=[[-1, 5 * P]], channel_multiplier=1).then_inc(const_done, 1)
            nc.gpsimd.affine_select(out=ident[:], in_=ones[:, 0:P], compare_op=ALU.is_equal, fill=0.0, base=0,
                                    pattern=[[-1, P]], channel_multiplier=1).then_inc(const_done, 1)
            nc.gpsimd.affine_select(out=ident16[:], in_=ones[:, 0:P], compare_op=ALU.is_equal, fill=0.0, base=0,
                                    pattern=[[-1, P]], channel_multiplier=1).then_inc(const_done, 1)
            for i in range(3):
                nc.gpsimd.memset(counts[:, i, :], 1.0 + i).then_inc(const_done, 1)
            pool.wait_ge(most_done, 7)
            nc.gpsimd.partition_all_reduce(most_all[:], most[:], P, RMAX).then_inc(all_done, 1)

            def value_sums(n):
                pool.wait_ge(v_out, n * TT + TT)
                nc.gpsimd.tensor_tensor(v_tail[:, 1], V[:, 2], V[:, 3], ALU.add).then_inc(vt_step, 1)
                pool.wait_ge(vt_step, n * 2 + 1)
                nc.gpsimd.tensor_tensor(v_tail[:, 0], v_tail[:, 1], V[:, 1], ALU.add).then_inc(vt_step, 1)

            pool.wait_ge(st_stored, 16 * (4 + NB))
            value_sums(0)

            def body(n, last):
                for r in range(NB // B):
                    nb = n * (NB // B) + r
                    if r > 0:
                        pool.wait_ge(pk_full, 2 * nb)
                    alone(pool, ld_pk, (nb + 1) * 48)
                    nc.gpsimd.tensor_copy(pk_16[:].rearrange("p a w -> p (a w)"),
                                          pk_in[:].rearrange("p a w -> p (a w)").bitcast(U8)
                                          .rearrange("p (c four) -> p c four", four=4)[:, :, 0]).then_inc(pk_conv, 1)
                if not last:
                    value_sums(n + 1)

            walk(body)(pool)

        @block.tensor
        def _(pe):
            def three(o, lhs, rhs, first, stop):
                pe.matmul(o, lhs(0), rhs(0), start=first, stop=False)
                pe.matmul(o, lhs(0), rhs(1), start=False, stop=False)
                return pe.matmul(o, lhs(1), rhs(0), start=False, stop=stop)

            def spread(st, n, banks):
                for k in range(KT):
                    for t in range(TT):
                        if st < 2:
                            src = xn[:, t, P * k:P * k + P]
                        else:
                            src = xn[:, t, 256 * (k // 2) + k % 2:256 * (k // 2) + 256:2]
                        mm = pe.transpose(bank[banks + k][:, P * t:P * t + P], src, ident[:])
                    mm.then_inc(spread_full[st], 1)

            def qkv(n):
                pe.wait_ge(spread_lo[0], n * KT + KT)
                for g in range(12):
                    bk = bank[g % 4]
                    if g >= 4:
                        pe.wait_ge(qk_lo, n * 8 + min(g - 3, 8))
                    for k in range(KT):
                        if g < 8:
                            w, c = g % 2, g // 2
                            mm = three(bk[:], lambda a: w_split[:, a, w, k, P * c:P * c + P], lambda a: xt[:, a, k, :], k == 0, k == KT - 1)
                        else:
                            s = g - 8
                            mm = three(bk[:], lambda a: xt[:, a, k, P * s:P * s + P], lambda a: w_split[:, a, 2, k, :], k == 0, k == KT - 1)
                    mm.then_inc(qkv_full, 1)

            def scores(n, u, j):
                hg, i = u // TT, u % TT
                if i == 0 and j == 0:
                    for g in (2 * hg, 2 * hg + 1):
                        pe.wait_ge(stacked[g % 4], n * 128 + 64 * (g // 4) + 64)
                if u > 0:
                    pe.wait_ge(exp_done, n * ROWS + 4 * (u - 1) + j + 1)
                h = 4 * hg + j
                pe.matmul(bank[j][:, 0:wide[i]], stack[:, 0, h, P * i:P * i + P], stack[:, 1, h, 0:wide[i]],
                          start=True, stop=True).then_inc(s_full, 1)

            def turn(n, u, j):
                i = u % TT
                pe.wait_ge(exp_done, n * ROWS + 4 * u + j + 1)
                if j >= 2:
                    pe.wait_ge(pt_act, n * 3 * UNITS + 3 * u + j - 1)
                elif u > 0:
                    if j == 0:
                        pe.wait_ge(pt_act, n * 3 * UNITS + 3 * u)
                    else:
                        pe.wait_ge(pt_dve, n * UNITS + u)
                    if i == 0:
                        pe.wait_ge((pk_out0, pk_out1)[j], n * (NB // B) + u // TT)
                for k in range(wide[i] // P):
                    mm = pe.transpose(bank[4 + j % 2][:, P * k:P * k + P], prob[:, u % 2, j, P * k:P * k + P], ident[:])
                mm.then_inc(t_full, 1)

            def values(n, u):
                hg, i = u // TT, u % TT
                pe.wait_ge(pt_act, n * 3 * UNITS + 3 * u + 3)
                pe.wait_ge(pt_dve, n * UNITS + u + 1)
                if u == 0:
                    pe.wait_ge(vt_step, n * 2 + 2)
                if u >= 2:
                    pe.wait_ge(o_step, n * 2 * UNITS + 2 * u - 2)
                blocks = wide[i] // P
                out_bank = bank[6 + u % 2]
                for what in range(2):
                    for k in range(blocks):
                        beyond = k == blocks - 1 and i < TT - 1
                        v = v_tail[:, i, :] if beyond and i < 2 else V[:, k, :]
                        for j in range(4):
                            h = 4 * hg + j
                            lhs = v[:, DH * h:DH * h + DH] if what == 0 else counts[:, TT - 2 - i if beyond else 0, :]
                            mm = pe.matmul(out_bank[32 * j:32 * j + 32, P * what:P * what + P], lhs,
                                           prob_t[:, u % 2, j, P * k:P * k + P], start=(k == 0), stop=(k == blocks - 1))
                mm.then_inc(av_done, 1)

            def out_proj(n):
                pe.wait_ge(o_lo, n * HG + HG)
                pe.wait_ge(pk_out0, (n + 1) * (NB // B))
                pe.wait_ge(pk_out1, (n + 1) * (NB // B))
                for t in range(TT):
                    for k in range(KT):
                        mm = three(bank[4 + t][:], lambda a: o_t[:, a, k, P * t:P * t + P], lambda a: w_split[:, a, 3, k, :], k == 0, k == KT - 1)
                    mm.then_inc(wo_full, 1)

            def mix(n):
                pe.wait_ge(spread_lo[1], n * KT + KT)
                pe.wait_ge(att_lo, n * KT + KT)
                for t in range(TT):
                    for k in range(KT):
                        mm = three(bank[t][:], lambda a: xt[:, a, k, P * t:P * t + P], lambda a: att_t[:, a, k, :], k == 0, k == KT - 1)
                    mm.then_inc(mix_full, 1)

            def context(n):
                pe.wait_ge(ld_ctx, n * 16 + 16)
                for cc in range(2):
                    for t in range(TT):
                        mm = pe.transpose(bank[4 + cc][:, P * t:P * t + P], c_in[:, t, P * cc:P * cc + P], ident[:])
                    mm.then_inc(ct_full, 1)
                pe.wait_ge(ct_done, n * 2 + 2)
                for i in range(2):
                    for cc in range(2):
                        mm = pe.matmul(bank[6 + i][:], xw_t[:, cc, i, :], c_t[:, cc, :], start=(cc == 0), stop=(cc == 1))
                    mm.then_inc(qkx_full, 1)
                pe.wait_ge(qkx_done, n * 2 + 2)
                for m in range(TT):
                    pe.matmul(bank[m][:], qk_x[:, 0, P * m:P * m + P], qk_x[:, 1, :], start=True, stop=True).then_inc(en_full, 1)
                pe.wait_ge(en_step, n * 5 + 5)
                for k in range(KT):
                    for m in range(TT):
                        mm = pe.transpose(bank[4 + k][:, P * m:P * m + P], e_p[:, m, P * k:P * k + P], ident[:])
                    mm.then_inc(att_full, 1)

            def repack(n, r):
                nb = n * (NB // B) + r
                pe.wait_ge(pk_conv, nb + 1)
                for half in range(2):
                    if half == 0:
                        pe.wait_ge(pt_act, n * 3 * UNITS + 3 * (TT * r + 3) + 3)
                    else:
                        pe.wait_ge(pt_dve, n * UNITS + TT * r + 4)
                    bk = bank[4 + half][:].bitcast(F16)
                    tiles = [[(0, 0), (1, 0)], [(0, 1), (1, 1)], [(2, 0), (3, 0)]] if half == 0 else \
                            [[(2, 1), (3, 1)], [(4, 0), (4, 1)], [(5, 0), (5, 1)]]
                    for q in range(3):
                        for e, (a, w) in enumerate(tiles[q]):
                            mm = pe.transpose(bk[:, 256 * q + P * e:256 * q + P * e + P], pk_16[:, a, P * w:P * w + P], ident16[:])
                    mm.then_inc(pk_full, 1)

            pe.wait_ge(const_done, 6)
            pe.wait_ge(ld_s, 48)
            for i in range(2):
                for q in range(8):
                    if i > 0:
                        pe.wait_ge(st_out, q + 1)
                    for e in range(4):
                        mm = pe.transpose(bank[q][0:16, P * e:P * e + P], gs_in[:, i, 4 * q + e, :], ident[:])
                    mm.then_inc(st_full, 1)
            pe.wait_ge(st_out, 9)
            for t in range(KT):
                mm = pe.transpose(bank[0][:, P * t:P * t + P], ds_in[:, t, :], ident[:])
            mm.then_inc(st_full, 1)
            pe.wait_ge(ld_small, 64)
            pe.wait_ge(st_out, 10)
            for cc in range(2):
                for i in range(2):
                    mm = pe.transpose(bank[1][:, 256 * cc + P * i:256 * cc + P * i + P], xw[:, i, P * cc:P * cc + P], ident[:])
            mm.then_inc(xw_full, 1)
            pe.wait_ge(st_out, 17)
            pe.wait_ge(xw_done, 1)
            pe.wait_ge(ln_done[0], 1)
            spread(0, 0, 0)
            pe.wait_ge(w_lo, 4)
            qkv(0)
            pe.wait_ge(v_out, TT)
            context(0)

            def body(n, last):
                pe.wait_ge(att_lo, n * KT + KT)
                for j in range(4):
                    scores(n, 0, j)
                for u in range(UNITS):
                    for j in range(4):
                        if u + 1 < UNITS:
                            scores(n, u + 1, j)
                        if j == 2 and u > 0:
                            values(n, u - 1)
                        turn(n, u, j)
                    if u % TT == TT - 1:
                        repack(n, u // TT)
                values(n, UNITS - 1)
                if not last:
                    pe.wait_ge(ln_done[0], n + 2)
                    pe.wait_ge(exp_done, (n + 1) * ROWS)
                    spread(0, n + 1, 0)
                out_proj(n)
                if not last:
                    qkv(n + 1)
                    pe.wait_ge(v_out, (n + 2) * TT)
                pe.wait_ge(ln_done[1], n + 1)
                spread(1, n, 4)
                mix(n)
                if not last:
                    pe.wait_ge(x2_done, n * TT + TT)
                    context(n + 1)
                    pe.wait_ge(en_exp, (n + 2) * TT)
                    pe.wait_ge(att_lo, (n + 2) * KT)
                else:
                    pe.wait_ge(x2_done, n * TT + TT)
                pe.wait_ge(ln_done[2], n + 1)
                spread(2, n, 4)
                pe.wait_ge(spread_lo[2], (n + 1) * KT)

            walk(body)(pe)

            def gate_up(it, par, s):
                g4 = 4 * ((it // 4) % 2)
                nbl, r = s // 2, s % 2
                if s == 0:
                    pe.wait_ge(in_xf[par], 16 * (it // 2) + 16)
                if s % 2 == 0:
                    pe.wait_ge(dq_lo, 4 * (it // 4) + 2 * nbl + 2)
                for which in range(2):
                    done = (g_full, u_full)[which]
                    bk = bank[2 * (s % 2) + which]
                    if not (isinstance(it, int) and it == 0 and s < 2):
                        pe.wait_ge((sq_out, int_out)[which], 4 * it + s - 1)
                    for k in range(KT):
                        kk, nib = k // 2, k % 2
                        if which == 0:
                            off, at = 0, 256 * kk
                        else:
                            off, at = (0, 512) if kk == 0 else (1, 0)
                        slot = g4 + 2 * nbl + off

                        def w(a):
                            if isinstance(slot, int):
                                return ring[:, a, slot, nib, at + P * r:at + P * r + P]
                            return ring[:, a, bass.ds(slot, 1), nib, at + P * r:at + P * r + P].rearrange("p a c -> p (a c)")
                        mm = three(bk[:], w, lambda a: xf[:, par, a, k, :], k == 0, k == KT - 1)
                    mm.then_inc(done, 1)

            def down(it, par, s):
                g4 = 4 * ((it // 4) % 2)
                nbl, r = s // 2, s % 2
                pe.wait_ge(hid_lo, 4 * it + s + 1)
                if s == 0 and not (isinstance(it, int) and it == 0):
                    pe.wait_ge(acc_out, it)
                slot = g4 + 2 * nbl + 1

                def w(a):
                    if isinstance(slot, int):
                        return ring[:, a, slot, r, 256:768]
                    return ring[:, a, bass.ds(slot, 1), r, 256:768].rearrange("p a c -> p (a c)")
                for t in range(TT):
                    mm = three(bank[4 + t][:], lambda a: hid[:, s % 2, a, P * t:P * t + P], w, s == 0, s == 3)
                mm.then_inc(down_done, 1)

            def iteration(it, par, nxt):
                for s in range(4):
                    if s < 3:
                        gate_up(it, par, s + 1)
                    elif nxt:
                        gate_up(it + 1, 1 - par, 0)
                    down(it, par, s)

            gate_up(0, 0, 0)
            iteration(0, 0, True)
            iteration(1, 1, True)
            with pe.Fori(1, 15) as i2:
                iteration(2 * i2, 0, True)
                iteration(2 * i2 + 1, 1, True)
            iteration(30, 0, True)
            iteration(31, 1, False)

        @block.scalar
        def _(act):
            def spread_heads(st, n, banks):
                for k in range(KT):
                    act.wait_ge(spread_full[st], n * KT + k + 1)
                    nc.scalar.activation(xt[:, 0, k, :], bank[banks + k][:], ACT.Copy, scale=XS).then_inc(spread_hi[st], 1)

            def qkv_heads(n):
                for g in range(12):
                    act.wait_ge(qkv_full, n * 12 + g + 1)
                    if g < 8:
                        if g >= 4:
                            act.wait_ge(qk_in[g % 4], n * 32 + 16)
                        elif not isinstance(n, int) or n > 0:
                            act.wait_ge(qk_in[g % 4], n * 32)
                        nc.scalar.activation(qk[:, g % 4, 0, :], bank[g % 4][:], ACT.Copy, scale=QS).then_inc(qk_hi, 1)
                    else:
                        nc.scalar.copy(V[:, g - 8, :], bank[g % 4][:]).then_inc(v_out, 1)

            def exp(n, u, j):
                i = u % TT
                act.wait_ge(shift_done, n * ROWS + 4 * u + j + 1)
                if u >= 2:
                    act.wait_ge(t_full, n * ROWS + 4 * (u - 2) + j + 1)
                nc.scalar.activation(prob[:, u % 2, j, 0:wide[i]], bank[j][:, 0:wide[i]], ACT.Exp,
                                     bias=nmx[:, u % 2, j:j + 1]).then_inc(exp_done, 1)

            def turned(n, u, j):
                i = u % TT
                act.wait_ge(t_full, n * ROWS + 4 * u + j + 1)
                if u >= 2:
                    act.wait_ge(av_done, n * UNITS + u - 1)
                nc.scalar.copy(prob_t[:, u % 2, j, 0:wide[i]], bank[4 + j % 2][:, 0:wide[i]]).then_inc(pt_act, 1)

            def out_head(n, hg):
                act.wait_ge(o_step, n * 2 * UNITS + 8 * hg + 8)
                nc.scalar.copy(o_t[:, 0, hg, :], o_sum[:]).then_inc(o_hi, 1)

            def repacked(n, r):
                nb = n * (NB // B) + r
                act.wait_ge(pk_full, 2 * nb + 1)
                if r > 0:
                    act.wait_ge(pk_stored, 32 * nb)
                nc.scalar.copy(pk_t[:, 0], bank[4][:].bitcast(F16)[:, 0:HALF]).then_inc(pk_out0, 1)

            def context(n):
                for cc in range(2):
                    act.wait_ge(ct_full, n * 2 + cc + 1)
                    nc.scalar.copy(c_t[:, cc, :], bank[4 + cc][:]).then_inc(ct_done, 1)
                for i in range(2):
                    act.wait_ge(qkx_full, n * 2 + i + 1)
                    nc.scalar.activation(qk_x[:, i, :], bank[6 + i][:], ACT.Identity, bias=xb[:, i:i + 1]).then_inc(qkx_done, 1)
                for m in range(TT):
                    act.wait_ge(en_max, n * TT + m + 1)
                    nc.scalar.activation(e_p[:, m, :], bank[m][:], ACT.Exp, bias=x_nm[:, m:m + 1],
                                         accum_out=x_den[:, m:m + 1]).then_inc(en_exp, 1)
                for k in range(KT):
                    act.wait_ge(att_full, n * KT + k + 1)
                    nc.scalar.copy(att_t[:, 0, k, :], bank[4 + k][:]).then_inc(att_hi, 1)

            act.wait_ge(fac_step, FAC_STEPS)
            act.wait_ge(ld_w, 64)
            for w in range(4):
                nc.scalar.activation(w_split[:, 0, w], w_raw[:, w], ACT.Copy, scale=fac[:, w:w + 1]).then_inc(w_hi, 1)
            for i in range(2):
                for q in range(8):
                    act.wait_ge(st_full, 8 * i + q + 1)
                    nc.scalar.activation(gu_st[i][:, 512 * q:512 * q + 512], bank[q][0:16, :], ACT.Copy,
                                         scale=(C_SG, C_SU)[i][0:16]).then_inc(st_out, 1)
            act.wait_ge(st_full, 17)
            nc.scalar.activation(d_st[:], bank[0][:], ACT.Copy, scale=C_SD).then_inc(st_out, 1)
            act.wait_ge(xw_full, 1)
            nc.scalar.copy(xw_t[:].rearrange("p a b c -> p (a b c)"), bank[1][:]).then_inc(xw_done, 1)
            spread_heads(0, 0, 0)
            qkv_heads(0)
            act.wait_ge(ld_small, 64)
            act.wait_ge(st_stored, 16 * (4 + NB))
            context(0)

            def body(n, last):
                for j in range(4):
                    if j == 0:
                        act.wait_ge(att_full, n * KT + KT)
                    exp(n, 0, j)
                for u in range(UNITS):
                    for j in range(4):
                        if u + 1 < UNITS:
                            exp(n, u + 1, j)
                        if j < 3:
                            turned(n, u, j)
                    if u % TT == TT - 1:
                        repacked(n, u // TT)
                    if u % TT == 1 and u > TT:
                        out_head(n, u // TT - 1)
                out_head(n, HG - 1)
                if not last:
                    act.wait_ge(xf_stored, n * 16 + 16)
                    spread_heads(0, n + 1, 0)
                    qkv_heads(n + 1)
                else:
                    act.wait_ge(xf_stored, n * 16 + 16)
                spread_heads(1, n, 4)
                if not last:
                    context(n + 1)
                spread_heads(2, n, 4)

            walk(body)(act)

            act.wait_ge(xf_stored, 16 * B + 16)
            act.wait_ge(pk_stored, 16 * 2 * NB)

            def dequant(hb, slot):
                act.wait_ge(dq_full, hb + 1)
                nc.scalar.copy(ring[:, 0, slot] if isinstance(slot, int) else ring[:, 0, bass.ds(slot, 1)].rearrange("p a b c -> p (a b) c"),
                               w_full[:]).then_inc(dq_hi, 1)

            def gate(it, s):
                q = s % 2
                step = 4 * it + s
                early = isinstance(it, int) and it == 0 and s < 2
                act.wait_ge(g_full, step + 1)
                if not early:
                    act.wait_ge(gel_out, step - 1)
                nc.scalar.activation(g_sb[:, q], bank[2 * q][:], ACT.Copy, scale=C_G).then_inc(g_out, 1)
                if not early:
                    act.wait_ge(cube_out, step - 1)
                nc.scalar.activation(sq[:, q], bank[2 * q][:], ACT.Square, scale=C_G).then_inc(sq_out, 1)
                act.wait_ge(cube_out, step + 1)
                nc.scalar.activation(th[:, q], cube[:, q], ACT.Tanh, scale=GELU_A * GELU_B).then_inc(th_out, 1)
                act.wait_ge(int_out, step + 1)
                if not early:
                    act.wait_ge(down_done, step - 1)
                nc.scalar.copy(hid[:, q, 0], inter[:, q]).then_inc(hid_hi, 1)

            def iteration(it, deq, nxt):
                for s in range(4):
                    if s < 3:
                        gate(it, s + 1)
                    elif nxt:
                        gate(it + 1, 0)
                    if s == 0 and deq:
                        if not isinstance(it, int) or it > 0:
                            act.wait_ge(down_done, 4 * it)
                        dequant(it + 4, (it + 4) % 8)

            for hb in range(4):
                dequant(hb, hb)
            gate(0, 0)
            iteration(0, True, True)
            with act.Fori(1, 28) as it:
                iteration(it, True, True)
            with act.Fori(28, 31) as it:
                iteration(it, False, True)
            iteration(31, False, False)

        @block.vector
        def _(dve):
            def norm(st, n):
                steps = Steps(dve, ln_step[st], n * LN_STEPS, LN_STEPS)
                tile = lambda t: X[:, t, :] if isinstance(t, int) else X[:, bass.ds(t, 1), :].rearrange("p a d -> p (a d)")
                for t in range(TT):
                    steps.mark(nc.vector.bn_stats(st6[:, t, :], tile(n * TT + t)))
                alone(dve, steps.sem, steps.base + steps.k)
                for t in range(TT):
                    steps.mark(nc.vector.bn_aggr(mv[:, t, :], st6[:, t, :]))
                steps.settle()
                steps.mark(nc.vector.tensor_scalar(var[:], mv[:, :, 1], EPS, None, ALU.add))
                steps.settle()
                steps.mark(nc.vector.tensor_scalar(rsi[:], var[:].bitcast(I32), 1, None, ALU.logical_shift_right))
                steps.settle()
                steps.mark(nc.vector.tensor_scalar(rs[:, 0].bitcast(I32), rsi[:], -1.0, float(0x5F3759DF), ALU.mult, ALU.add))
                for _ in range(3):
                    steps.settle()
                    steps.mark(nc.vector.tensor_tensor(rs[:, 1], rs[:, 0], rs[:, 0], ALU.mult))
                    steps.settle()
                    steps.mark(nc.vector.scalar_tensor_tensor(rs[:, 1], rs[:, 1], -0.5, var[:], ALU.mult, ALU.mult))
                    steps.settle()
                    steps.mark(nc.vector.scalar_tensor_tensor(rs[:, 0], rs[:, 1], 1.5, rs[:, 0], ALU.add, ALU.mult))
                steps.settle()
                for t in range(TT):
                    ins = nc.vector.tensor_scalar(xn[:, t, :], tile(n * TT + t), mv[:, t, 0:1], rs[:, 0, t:t + 1], ALU.subtract, ALU.mult)
                ins.then_inc(ln_done[st], 1)
                steps.end()

            def spread_tails(st, n, banks):
                for k in range(KT):
                    dve.wait_ge(spread_hi[st], n * KT + k + 1)
                    nc.vector.scalar_tensor_tensor(xt[:, 1, k, :], bank[banks + k][:], XS, xt[:, 0, k, :],
                                                   ALU.mult, ALU.subtract).then_inc(spread_lo[st], 1)

            def qkv_tails(n):
                for g in range(8):
                    dve.wait_ge(qk_hi, n * 8 + g + 1)
                    nc.vector.scalar_tensor_tensor(qk[:, g % 4, 1, :], bank[g % 4][:], QS, qk[:, g % 4, 0, :],
                                                   ALU.mult, ALU.subtract).then_inc(qk_lo, 1)

            def row_max(n, u, j):
                i = u % TT
                alone(dve, s_full, n * ROWS + 4 * u + j + 1)
                nc.vector.tensor_tensor_reduce(out=bank[j][:, 0:wide[i]], in0=bank[j][:, 0:wide[i]],
                                               in1=mask[:, P * (3 - i):P * (3 - i) + wide[i]], scale=C_EXP,
                                               scalar=0.0 if i < TT - 1 else NEG, op0=ALU.mult, op1=ALU.max,
                                               accum_out=mx[:, u % 2, j:j + 1]).then_inc(max_done, 1)

            def shift(n, u, j):
                dve.wait_ge(max_done, n * ROWS + 4 * u + j + 1)
                nc.vector.tensor_scalar(nmx[:, u % 2, j:j + 1], mx[:, u % 2, j:j + 1], -1.0, None, ALU.mult).then_inc(shift_done, 1)

            def turned(n, u):
                i = u % TT
                dve.wait_ge(t_full, n * ROWS + 4 * u + 4)
                if u >= 2:
                    dve.wait_ge(av_done, n * UNITS + u - 1)
                nc.vector.tensor_copy(prob_t[:, u % 2, 3, 0:wide[i]], bank[5][:, 0:wide[i]]).then_inc(pt_dve, 1)

            def divide(n, u):
                hg, i = u // TT, u % TT
                dve.wait_ge(av_done, n * UNITS + u + 1)
                nc.vector.reciprocal(r_den[:, u % 2, :], bank[6 + u % 2][:, P:2 * P]).then_inc(o_step, 1)
                if i == 0 and hg > 0:
                    dve.wait_ge(o_hi, n * HG + hg)
                    dve.wait_ge(o_lo, n * HG + hg)
                dve.wait_ge(o_step, n * 2 * UNITS + 2 * u + 1)
                nc.vector.scalar_tensor_tensor(o_sum[:, P * i:P * i + P], bank[6 + u % 2][:, 0:P], QS, r_den[:, u % 2, :],
                                               ALU.mult, ALU.mult).then_inc(o_step, 1)

            def out_tail(n, hg):
                dve.wait_ge(o_hi, n * HG + hg + 1)
                nc.vector.tensor_tensor(o_t[:, 1, hg, :], o_sum[:], o_t[:, 0, hg, :], ALU.subtract).then_inc(o_lo, 1)

            def repacked(n, r):
                nb = n * (NB // B) + r
                dve.wait_ge(pk_full, 2 * nb + 2)
                if r > 0:
                    dve.wait_ge(pk_stored, 32 * nb)
                nc.vector.tensor_copy(pk_t[:, 1], bank[5][:].bitcast(F16)[:, 0:HALF]).then_inc(pk_out1, 1)

            def residual(n, full, banks, factor, done):
                for t in range(TT):
                    dve.wait_ge(full, n * TT + t + 1)
                    at = n * TT + t
                    xv = X[:, at, :] if isinstance(at, int) else X[:, bass.ds(at, 1), :].rearrange("p a d -> p (a d)")
                    nc.vector.scalar_tensor_tensor(xv, bank[banks + t][:], factor, xv, ALU.mult, ALU.add).then_inc(done, 1)
                alone(dve, done, n * TT + TT)

            def context(n):
                for m in range(TT):
                    dve.wait_ge(en_full, n * TT + m + 1)
                    nc.vector.tensor_reduce(x_nm[:, m:m + 1], bank[m][:], AX.X, ALU.max, negate=True).then_inc(en_max, 1)
                dve.wait_ge(en_exp, n * TT + TT)
                nc.vector.reciprocal(x_rden[:], x_den[:]).then_inc(en_step, 1)
                dve.wait_ge(en_step, n * 5 + 1)
                for m in range(TT):
                    nc.vector.tensor_scalar(e_p[:, m, :], e_p[:, m, :], x_rden[:, m:m + 1], AS, ALU.mult, ALU.mult).then_inc(en_step, 1)

            def context_tails(n):
                for k in range(KT):
                    dve.wait_ge(att_hi, n * KT + k + 1)
                    nc.vector.tensor_tensor(att_t[:, 1, k, :], bank[4 + k][:], att_t[:, 0, k, :], ALU.subtract).then_inc(att_lo, 1)

            dve.wait_ge(ld_w, 64)
            for w in range(4):
                nc.vector.tensor_reduce(most[:, w:w + 1], w_raw[:, w].rearrange("p k n -> p (k n)"), AX.X, ALU.max,
                                        apply_absolute_value=True).then_inc(most_done, 1)
            dve.wait_ge(ld_s, 48)
            for i in range(2):
                nc.vector.tensor_reduce(most[:, SG + i:SG + i + 1], gs_in[:, i].rearrange("p n k -> p (n k)"), AX.X, ALU.max,
                                        apply_absolute_value=True).then_inc(most_done, 1)
            nc.vector.tensor_reduce(most[:, SD:SD + 1], ds_in[:].rearrange("p t k -> p (t k)"), AX.X, ALU.max,
                                    apply_absolute_value=True).then_inc(most_done, 1)
            dve.wait_ge(ld_x0, 16)
            norm(0, 0)
            dve.wait_ge(all_done, 1)
            steps = Steps(dve, fac_step, 0, FAC_STEPS)
            e0, e1 = expo[:, 0], expo[:, 1]
            steps.mark(nc.vector.tensor_scalar(e0, most_all[:].bitcast(I32), 23, None, ALU.logical_shift_right))
            steps.settle()
            steps.mark(nc.vector.tensor_scalar(e1, e0, -1.0, float(TOP + 127), ALU.mult, ALU.add))
            steps.settle()
            steps.mark(nc.vector.tensor_scalar(e0, e1, float(CAP), None, ALU.min))
            steps.settle()
            steps.mark(nc.vector.tensor_scalar(fac[:].bitcast(I32), e0, 23, None, ALU.logical_shift_left))
            steps.mark(nc.vector.tensor_scalar(e1, e0, -1.0, 254.0, ALU.mult, ALU.add))
            steps.settle()
            steps.mark(nc.vector.tensor_scalar(ifac[:].bitcast(I32), e1, 23, None, ALU.logical_shift_left))
            steps.settle()

            def pair(dst, a, s, b):
                steps.mark(nc.vector.scalar_tensor_tensor(dst, a, s, b, ALU.mult, ALU.mult))

            def one(dst, a, s):
                steps.mark(nc.vector.tensor_scalar(dst, a, s, None, ALU.mult))

            f = lambda i: fac[:, i:i + 1]
            r = lambda i: ifac[:, i:i + 1]
            pair(C_EXP, r(0), 2.0 ** 14 / float(np.sqrt(T)), r(1))
            pair(C_NEXP, r(0), -(2.0 ** 14) / float(np.sqrt(T)), r(1))
            pair(C_O, r(2), 2.0 ** 7, r(3))
            one(C_G, r(SG), 1.0 / XS)
            one(C_I, f(SG), 2.0 ** -46)
            pair(tmpc[:, 0:1], r(SG), 2.0 ** 34, r(SU))
            one(C_SG, f(SG), LUT)
            one(C_SU, f(SU), LUT)
            one(C_SD, f(SD), LUT)
            steps.settle()
            steps.mark(nc.vector.tensor_tensor(C_OUT, tmpc[:, 0:1], r(SD), ALU.mult))
            steps.settle()
            steps.end()
            for w in range(4):
                dve.wait_ge(w_hi, w + 1)
                nc.vector.scalar_tensor_tensor(w_split[:, 1, w], w_raw[:, w], fac[:, w:w + 1], w_split[:, 0, w],
                                               ALU.mult, ALU.subtract).then_inc(w_lo, 1)
            spread_tails(0, 0, 0)
            dve.wait_ge(w_lo, 4)
            qkv_tails(0)
            context(0)
            context_tails(0)
            dve.wait_ge(const_done, 6)
            dve.wait_ge(ld_x, 16 * (B - 1))

            def body(n, last):
                if not last:
                    norm(0, n + 1)
                for j in range(4):
                    row_max(n, 0, j)
                    if j > 0:
                        shift(n, 0, j - 1)
                shift(n, 0, 3)
                for u in range(UNITS):
                    nxt = u + 1 < UNITS
                    for j in range(4):
                        if u > 0 and j == 0:
                            turned(n, u - 1)
                            if u % TT == 0:
                                repacked(n, u // TT - 1)
                        if nxt:
                            row_max(n, u + 1, j)
                            if j > 0:
                                shift(n, u + 1, j - 1)
                        if j == 1 and u % TT == 2 and u > TT:
                            out_tail(n, u // TT - 1)
                        if u > 1 and j == 2:
                            divide(n, u - 2)
                    if nxt:
                        shift(n, u + 1, 3)
                turned(n, UNITS - 1)
                repacked(n, HG - 1)
                divide(n, UNITS - 2)
                divide(n, UNITS - 1)
                out_tail(n, HG - 1)
                if not last:
                    spread_tails(0, n + 1, 0)
                residual(n, wo_full, 4, C_O, x1_done)
                norm(1, n)
                if not last:
                    qkv_tails(n + 1)
                spread_tails(1, n, 4)
                residual(n, mix_full, 0, 1.0 / (XS * AS), x2_done)
                norm(2, n)
                if not last:
                    context(n + 1)
                    context_tails(n + 1)
                spread_tails(2, n, 4)

            walk(body)(dve)

            dve.wait_ge(xf_stored, 16 * B + 16)
            dve.wait_ge(pk_stored, 16 * 2 * NB)

            def dequant(hb, slot, par):
                steps = Steps(dve, dq_step, hb * 6, 6)
                dve.wait_ge(in_pk[par], 32 * (hb // 2) + 32)
                words = pk_in2[:, par].bitcast(U32)
                for nib in range(2):
                    steps.mark(nc.vector.tensor_scalar(bits[:, nib], words, 9 - 4 * nib, 0x0E000E00,
                                                       ALU.logical_shift_left, ALU.bitwise_and))
                    steps.mark(nc.vector.tensor_scalar(codes[:, nib], words, 12 - 4 * nib, 0x80008000,
                                                       ALU.logical_shift_left, ALU.bitwise_and))
                steps.settle()
                for nib in range(2):
                    steps.mark(nc.vector.tensor_tensor(codes[:, nib], codes[:, nib], bits[:, nib], ALU.bitwise_or))
                steps.settle()
                steps.end()
                if not isinstance(hb, int) or hb > 0:
                    dve.wait_ge(dq_lo, hb)
                sc = sc_in[:, par]
                nc.vector.tensor_tensor(w_full[:], codes[:].rearrange("p a c -> p (a c)").bitcast(F16).rearrange("p (a c) -> p a c", a=2),
                                        sc.unsqueeze(1).to_broadcast([P, 2, HALF]), ALU.mult).then_inc(dq_full, 1)
                dve.wait_ge(dq_hi, hb + 1)
                lo, hi = (ring[:, a, slot] if isinstance(slot, int) else ring[:, a, bass.ds(slot, 1)].rearrange("p a b c -> p (a b) c") for a in (1, 0))
                nc.vector.tensor_tensor(lo, w_full[:], hi, ALU.subtract).then_inc(dq_lo, 1)

            def gate(it, s):
                q = s % 2
                step = 4 * it + s
                early = isinstance(it, int) and it == 0 and s < 2
                dve.wait_ge(sq_out, step + 1)
                if not early:
                    dve.wait_ge(th_out, step - 1)
                nc.vector.scalar_tensor_tensor(cube[:, q], sq[:, q], 1.0 / GELU_B, g_sb[:, q], ALU.add, ALU.mult).then_inc(cube_out, 1)
                dve.wait_ge(th_out, step + 1)
                nc.vector.scalar_tensor_tensor(gel[:, q], th[:, q], 1.0, g_sb[:, q], ALU.add, ALU.mult).then_inc(gel_out, 1)
                dve.wait_ge(gel_out, step + 1)
                dve.wait_ge(u_full, step + 1)
                nc.vector.scalar_tensor_tensor(inter[:, q], bank[2 * q + 1][:], C_I, gel[:, q], ALU.mult, ALU.mult).then_inc(int_out, 1)
                dve.wait_ge(hid_hi, step + 1)
                nc.vector.tensor_tensor(hid[:, q, 1], inter[:, q], hid[:, q, 0], ALU.subtract).then_inc(hid_lo, 1)

            def add_out(it):
                dve.wait_ge(down_done, 4 * it + 4)
                for t in range(TT):
                    at = (it % B) * TT + t
                    xv = X[:, at, :] if isinstance(at, int) else X[:, bass.ds(at, 1), :].rearrange("p a d -> p (a d)")
                    ins = nc.vector.scalar_tensor_tensor(xv, bank[4 + t][:], C_OUT, xv, ALU.mult, ALU.add)
                ins.then_inc(acc_out, 1)

            def iteration(it, par, deq, nxt):
                for s in range(4):
                    if s < 3:
                        gate(it, s + 1)
                    elif nxt:
                        gate(it + 1, 0)
                    if s == 0 and deq:
                        dequant(it + 4, (it + 4) % 8, par)
                add_out(it)

            for hb in range(4):
                dequant(hb, hb, hb % 2)
            gate(0, 0)
            iteration(0, 0, True, True)
            iteration(1, 1, True, True)
            with dve.Fori(1, 14) as i2:
                iteration(2 * i2, 0, True, True)
                iteration(2 * i2 + 1, 1, True, True)
            with dve.Fori(28, 31) as it:
                iteration(it, 0, False, True)
            iteration(31, 1, False, False)


FAC_STEPS = 6 + 10
GELU_A = 0.7978845608028654
GELU_B = 0.044715

_INS = ["x", "ctx_1024", "L0_attn_Wq", "L0_attn_Wk", "L0_attn_Wv", "L0_attn_Wo", "L0_xattn_Wq", "L0_xattn_bq",
        "L0_xattn_Wk", "L0_xattn_bk", "L0_ffn_gate_W_packed", "L0_ffn_gate_scales", "L0_ffn_up_W_packed",
        "L0_ffn_up_scales", "L0_ffn_down_W_packed", "L0_ffn_down_scales"]
_OUTS = [((4, 512, 512), "float32")]


def kernel(**inputs):
    import numpy as _np
    import concourse.bacc as _bacc
    from concourse import mybir as _mybir
    from concourse.bass_utils import run_bass_kernel_spmd as _run

    nc = _bacc.Bacc("TRN2", target_bir_lowering=False, num_devices=1)
    arrays, args = {}, []
    for name in _INS:
        a = _np.ascontiguousarray(inputs[name])
        arrays[f"in_{name}_dram"] = a
        args.append(nc.dram_tensor(f"in_{name}_dram", a.shape, _mybir.dt.from_np(a.dtype), kind="ExternalInput").ap())
    for i, (shape, dtype) in enumerate(_OUTS):
        dt = _mybir.dt.from_np(_np.dtype(dtype))
        args.append(nc.dram_tensor(f"out_{i}_dram", shape, dt, kind="ExternalOutput").ap())
    decoder_layer(nc, *args)
    r = _run(nc, [arrays], core_ids=[0])
    got = tuple(r.results[0][f"out_{i}_dram"] for i in range(len(_OUTS)))
    return got[0]
```

```python
from contextlib import ExitStack

import numpy as np

import concourse.bass as bass
from concourse import mybir

F32 = mybir.dt.float32
F16 = mybir.dt.float16
I32 = mybir.dt.int32
U32 = mybir.dt.uint32
I16 = mybir.dt.int16
U8 = mybir.dt.uint8
ALU = mybir.AluOpType
ACT = mybir.ActivationFunctionType
AX = mybir.AxisListType
RMAX = bass.bass_isa.ReduceOp.max

P = 128
B, T, D = 4, 512, 512
HEADS, DH = 16, 32
C, DX = 256, 128
F = 4096
QBLOCK = 32
TT = T // P
KT = D // P
HG = HEADS // 4
UNITS = HG * TT
NB = F // 256
HALF = 768
EPS = 1e-5

XS = 2.0 ** 11
QS = 2.0 ** -18
AS = 2.0 ** 14
TOP = 127 + 12
CAP = 127 + 60
LUT = 2.0 ** 14
NEG = -3.0e38

WEIGHTS = ("q", "k", "v", "o")
SG, SU, SD = 4, 5, 6


class Steps:

    def __init__(self, eng, sem, base, per):
        self.eng, self.sem, self.base, self.per, self.k = eng, sem, base, per, 0

    def mark(self, ins):
        ins.then_inc(self.sem, 1)
        self.k += 1

    def settle(self):
        self.eng.wait_ge(self.sem, self.base + self.k)

    def end(self):
        assert self.k == self.per, (self.k, self.per)


def decoder_layer(nc, x, ctx_1024, Wq, Wk, Wv, Wo, xWq, xbq, xWk, xbk, gate_p, gate_s, up_p, up_s, down_p, down_s, out):
    with ExitStack() as ctx:
        def sem(name):
            return ctx.enter_context(nc.semaphore(name))

        def psum(name, shape, dt):
            return ctx.enter_context(nc.psum_tensor(name, shape, dt))

        def keep(name, shape, dt):
            return ctx.enter_context(nc.sbuf_tensor(name, shape, dt))

        packed_t = nc.dram_tensor("packed_t", (2 * NB, P, HALF), I16, kind="Internal").ap()
        scale_t = nc.dram_tensor("scale_t", (2 * NB, 8, HALF), F32, kind="Internal").ap()
        qk_dram = nc.dram_tensor("qk_dram", (2, 2, D, T), F16, kind="Internal").ap()
        xf_dram = nc.dram_tensor("xf_dram", (B, P, 2 * KT * T), F16, kind="Internal").ap()

        bank = [psum(f"bank{i}", [P, 512], F32) for i in range(8)]
        X = keep("X", [P, B * TT, D], F32)
        fac = keep("fac", [P, 7], F32)
        ifac = keep("ifac", [P, 7], F32)
        col = keep("col", [P, 12], F32)
        C_EXP, C_O, C_G, C_I, C_OUT, C_SG, C_SU, C_SD = (col[:, i:i + 1] for i in range(8))
        tmpc = keep("tmpc", [P, 4], F32)

        first = ExitStack()

        def sb(name, shape, dt):
            return first.enter_context(nc.sbuf_tensor(name, shape, dt))

        w_split = sb("w_split", [P, 4, 2, KT, D], F16)
        prob = sb("prob", [P, 2, 4, T], F32)
        qk = sb("qk", [P, 4, 2, T], F16)
        xt = sb("xt", [P, 2, KT, T], F16)
        c_in = sb("c_in", [P, TT, C], F32)
        stack = sb("stack", [P, 2, HEADS, T], F16)
        prob_t = sb("prob_t", [P, 2, 4, T], F32)
        V = sb("V", [P, TT, D], F32)
        v_beyond = sb("v_beyond", [P, TT - 1, D], F32)
        w_raw = stack[:].rearrange("p a h t -> p (a h t)").bitcast(F32).rearrange("p (w k n) -> p w k n", w=4, k=KT)
        xn = sb("xn", [P, TT, D], F32)
        o_t = sb("o_t", [P, 2, HG, T], F16)
        att_t = sb("att_t", [P, 2, KT, T], F16)
        c_t = prob_t[:, 0, 0:2, :]
        qk_x = prob_t[:, 1, 0:2, :]
        e_p = prob[:, 1, :, :]
        xw_t = sb("xw_t", [P, 2, 2, DX], F32)
        xb = sb("xb", [P, 2], F32)
        o_sum = sb("o_sum", [P, T], F32)
        den = sb("den", [P, 2, 4], F32)
        den_all = sb("den_all", [P, 2, 4], F32)
        r_col = sb("r_col", [P, 2, 4], F32)
        r_den = sb("r_den", [P, 2, P], F32)
        e_zero = sb("e_zero", [P, 2, 4], F32)
        v_zero = sb("v_zero", [P, 2, P], F32)
        mask = sb("mask", [P, T], F32)
        ident = sb("ident", [P, P], F32)
        ident16 = sb("ident16", [P, P], F16)
        ones = V[:].rearrange("p t d -> p (t d)")[:, 0:T]
        o_raw = o_t[:].rearrange("p a h t -> p (a h t)").bitcast(F32)
        gs_in = o_raw[:, 0:1024].rearrange("p (i n k) -> p i n k", i=2, k=D // QBLOCK)
        ds_in = o_raw[:, 1024:1536].rearrange("p (t k) -> p t k", t=KT)
        gu_st = [tuple(X[0:16, t:t + TT].rearrange("p t d -> p (t d)") for t in (2 * TT, 3 * TT)),
                 (prob[0:16, 0].rearrange("p j t -> p (j t)"), att_t[0:16].rearrange("p a k t -> p (a k t)").bitcast(F32))]
        d_st = v_beyond[:, 0]
        xw = v_beyond[:, 1].rearrange("p (i c) -> p i c", i=2)
        most = sb("most", [P, 7], F32)
        most_all = sb("most_all", [P, 7], F32)
        expo = sb("expo", [P, 2, 7], I32)
        pk_in = sb("pk_in", [P, 6, C], I32)
        pk_16 = sb("pk_16", [P, 6, C], F16)
        pk_t = sb("pk_t", [P, 2, HALF], I16)
        st6 = sb("st6", [P, TT, 6], F32)
        mv = sb("mv", [P, TT, 2], F32)
        var = sb("var", [P, TT], F32)
        rs = sb("rs", [P, 2, TT], F32)
        rsi = sb("rsi", [P, TT], I32)
        mx = sb("mx", [P, 2, 4], F32)
        nmx = sb("nmx", [P, 2, 4], F32)
        x_nm = sb("x_nm", [P, 4], F32)
        x_den = sb("x_den", [P, 4], F32)
        x_rden = sb("x_rden", [P, 4], F32)
        first.close()

        second = ExitStack()

        def sb2(name, shape, dt):
            return second.enter_context(nc.sbuf_tensor(name, shape, dt))

        ring = sb2("ring", [P, 8, 2, 2, HALF], F16)
        pk_in2 = sb2("pk_in2", [P, 2, HALF], I16)
        sc_in = sb2("sc_in", [P, 2, HALF], F32)
        bits = sb2("bits", [P, HALF // 2], U32)
        codes = sb2("codes", [P, 2, HALF // 2], U32)
        w_full = sb2("w_full", [P, 2, HALF], F32)
        xf = sb2("xf", [P, 2, 2, KT, T], F16)
        g_sb = sb2("g_sb", [P, 2, T], F32)
        sq = sb2("sq", [P, 2, T], F32)
        cube = sb2("cube", [P, 2, T], F32)
        th = sb2("th", [P, 2, T], F32)
        gel = sb2("gel", [P, 2, T], F32)
        inter = sb2("inter", [P, 2, T], F32)
        hid = sb2("hid", [P, 2, 2, T], F16)
        second.close()

        ld_w = [sem(f"ld_w{w}") for w in range(4)]
        ld_s, ld_x0, ld_x1, ld_x, ld_small = (sem(n) for n in ("ld_s", "ld_x0", "ld_x1", "ld_x", "ld_small"))
        ld_ctx, ld_pk = sem("ld_ctx"), sem("ld_pk")
        const_ones, const_done = sem("const_ones"), sem("const_done")
        most_done, all_done, fac_step = sem("most_done"), sem("all_done"), sem("fac_step")
        w_hi, w_lo = sem("w_hi"), sem("w_lo")
        st_full, st_out, st_scaled = (sem(n) for n in ("st_full", "st_out", "st_scaled"))
        sg_stored, su_stored, sd_stored = (sem(n) for n in ("sg_stored", "su_stored", "sd_stored"))
        xw_full, xw_done = sem("xw_full"), sem("xw_done")
        ln_step = [sem(f"ln{i}_step") for i in range(3)]
        ln_done = [sem(f"ln{i}_done") for i in range(3)]
        spread_full = [sem(f"spread{i}_full") for i in range(3)]
        spread_hi = [sem(f"spread{i}_hi") for i in range(3)]
        spread_lo = [sem(f"spread{i}_lo") for i in range(3)]
        qkv_full, qk_hi, qk_lo, v_out = (sem(n) for n in ("qkv_full", "qk_hi", "qk_lo", "v_out"))
        vb_full, vb_out, e_zero_done, v_zero_done = (sem(n) for n in ("vb_full", "vb_out", "e_zero_done", "v_zero_done"))
        stacked = [sem(f"stacked{i}") for i in range(4)]
        s_full, max_done, shift_done, exp_done = (sem(n) for n in ("s_full", "max_done", "shift_done", "exp_done"))
        qk_in, t_full = [sem(f"qk_in{i}") for i in range(4)], sem("t_full")
        pt_act, pt_dve, av_done, o_done, o_hi, o_lo = (sem(n) for n in ("pt_act", "pt_dve", "av_done", "o_done", "o_hi", "o_lo"))
        den_done, rcol_done, r_full, rden_out = (sem(n) for n in ("den_done", "rcol_done", "r_full", "rden_out"))
        wo_full, x1_done, mix_full, x2_done = (sem(n) for n in ("wo_full", "x1_done", "mix_full", "x2_done"))
        ct_full, ct_done, qkx_full, qkx_done = (sem(n) for n in ("ct_full", "ct_done", "qkx_full", "qkx_done"))
        en_full, en_max, en_exp, en_step, att_full, att_hi, att_lo = (
            sem(n) for n in ("en_full", "en_max", "en_exp", "en_step", "att_full", "att_hi", "att_lo"))
        pk_conv, pk_full, pk_out0, pk_out1, pk_stored = (sem(n) for n in ("pk_conv", "pk_full", "pk_out0", "pk_out1", "pk_stored"))
        xf_stored = sem("xf_stored")
        in_pk, in_xf = [sem("in_pk0"), sem("in_pk1")], [sem("in_xf0"), sem("in_xf1")]
        dq_step, dq_full, dq_hi, dq_lo = (sem(n) for n in ("dq_step", "dq_full", "dq_hi", "dq_lo"))
        g_full, u_full, sq_out, cube_out, th_out = (sem(n) for n in ("g_full", "u_full", "sq_out", "cube_out", "th_out"))
        gel_out, int_out, hid_hi, hid_lo, down_done, acc_out = (
            sem(n) for n in ("gel_out", "int_out", "hid_hi", "hid_lo", "down_done", "acc_out"))
        out_stored, passed = sem("out_stored"), sem("passed")

        LN_PARTS = 2 * TT + 3 + 9 + TT
        ROWS = 4 * UNITS
        wide = [(i + 1) * P for i in range(TT)]

        def turn_slot(h):
            return h + 2 * (max(0, h - 2) // 16) + max(0, h // 4 - 1)

        def pack_slot(r, half):
            return (turn_slot(16 * r + 17) + 1 if r < HG - 1 else recip_slot(UNITS - 2) + 1) + half

        def recip_slot(u):
            return turn_slot(4 * u + 7) + 1 if u < UNITS - 1 else pack_slot(HG - 1, 1) + 1

        def turn_bank(slot):
            return bank[(4, 5, 7)[slot % 3]]

        def turn_read(n, slot):
            for u in range(UNITS):
                if slot == recip_slot(u):
                    return rden_out, n * UNITS + u + 1
                for j in range(4):
                    if slot == turn_slot(4 * u + j):
                        return (pt_act, n * 3 * UNITS + 3 * u + j + 1) if j < 3 else (pt_dve, n * UNITS + u + 1)
            r, half = next((r, half) for r in range(HG) for half in range(2) if slot == pack_slot(r, half))
            return (pk_out0, pk_out1)[half], n * (NB // B) + r + 1

        AHEAD = 3
        AT_RECIP, AT_DIVIDE = 9, 12
        AT_SUMS, AT_TURNED, AT_RECIPROCALS = 1, 3, 2
        AT_OUT = 0

        def beyond_units(n, u):
            return n * HG * (TT - 1) + u // TT * (TT - 1) + min(u % TT + 1, TT - 1)

        def alone(eng, sem, value):
            eng.wait_ge(sem, value)
            eng.sem_inc(passed, 1)

        def walk(body):
            def run(eng):
                with eng.Fori(0, B - 1) as n:
                    body(n, False)
                body(B - 1, True)
            return run

        block = ctx.enter_context(nc.Block())

        @block.sync
        def _(sp):
            sp.sem_inc(xf_stored, 16)
            sp.dma_start(X[:, 0:TT, :], x[0].rearrange("(t p) d -> p t d", p=P)).then_inc(ld_x0, 16)
            for i, src in enumerate((gate_s, up_s)):
                sp.dma_start(gs_in[:, i].rearrange("p (n r) k -> p n (r k)", r=2),
                             src.rearrange("(n p r) k -> p n (r k)", p=P, r=2)).then_inc(ld_s, 16)
            sp.dma_start(ds_in[:], down_s.rearrange("(t p) k -> p t k", p=P)).then_inc(ld_s, 16)
            for w, src in enumerate((Wq, Wk, Wv, Wo)):
                sp.dma_start(w_raw[:, w], src.rearrange("(k p) n -> p k n", p=P)).then_inc(ld_w[w], 16)
            for i, (w, bv) in enumerate(((xWq, xbq), (xWk, xbk))):
                sp.dma_start(xw[:, i], w).then_inc(ld_small, 16)
                sp.dma_start(xb[:, i:i + 1], bv.rearrange("(p a) -> p a", a=1)).then_inc(ld_small, 16)

            def load_x(b):
                sp.dma_start(X[:, b * TT:(b + 1) * TT, :], x[b].rearrange("(t p) d -> p t d", p=P)).then_inc(ld_x1 if b == 1 else ld_x, 16)

            def load_ctx(n):
                if not isinstance(n, int) or n > 0:
                    sp.wait_ge(ct_full, n * 2)
                sp.dma_start(c_in[:], ctx_1024[n].rearrange("(t p) c -> p t c", p=P) if isinstance(n, int)
                             else ctx_1024[bass.ds(n, 1)].rearrange("a (t p) c -> p (a t) c", p=P)).then_inc(ld_ctx, 16)

            def stack_heads(n, groups):
                def fetch(g):
                    c, which = g // 2, g % 2
                    sp.wait_ge(qk_in[g % 4], n * 32 + 16 * (g // 4) + 16)
                    for part in range(4):
                        hl = part % 2 if which == 0 else part // 2
                        sp.dma_start(stack[32 * part:32 * part + 32, which, 4 * c:4 * c + 4, :],
                                     qk_dram[which, hl, P * c:P * c + P, :].rearrange("(j d) t -> d j t", d=DH)).then_inc(stacked[g % 4], 16)

                for g in groups:
                    c, which = g // 2, g % 2
                    sp.wait_ge(qk_lo, n * 2 * HG + g + 1)
                    sp.dma_start(qk_dram[which, :, P * c:P * c + P, :].rearrange("a p t -> p a t"), qk[:, g % 4]).then_inc(qk_in[g % 4], 16)
                    if g > groups[0]:
                        fetch(g - 1)
                fetch(groups[-1])

            load_ctx(0)
            load_x(1)

            def store_scales(i):
                sp.wait_ge(st_scaled, (5, 2)[i])
                for kk in range(2):
                    hb, piece = (0, kk) if i == 0 else (kk, 2 * (1 - kk))
                    for half in range(2):
                        dst = scale_t[NB * half:NB * half + NB].rearrange("(n a) k c -> k n a c", a=2)[:, :, hb, 256 * piece:256 * piece + 256]
                        sp.dma_start(dst, gu_st[i][half][8 * kk:8 * kk + 8, :].rearrange("k (n c) -> k n c", n=NB // 2)).then_inc((sg_stored, su_stored)[i], 16)

            sp.wait_ge(w_lo, 4)
            stack_heads(0, (0, 1, 2, 3))
            stack_heads(0, (4, 5, 6, 7))
            store_scales(1)
            sp.wait_ge(st_scaled, 3)
            for nb in range(NB):
                sp.dma_start(scale_t[2 * nb + 1, :, 256:768], d_st[8 * nb:8 * nb + 8, :]).then_inc(sd_stored, 16)
            store_scales(0)
            sp.wait_ge(sg_stored, 16 * 4)
            for b in range(2, B):
                load_x(b)

            def load_half(hb, slot, ready):
                sp.dma_start(pk_in2[:, slot], packed_t[bass.ds(hb, 1)].rearrange("a p c -> p (a c)")).then_inc(in_pk[ready], 16)
                rows = scale_t[bass.ds(hb, 1)]
                sp.dma_start(sc_in[:, slot], bass.AP(rows.tensor, rows.offset, [[HALF, 8], [0, 16], [1, HALF]])).then_inc(in_pk[ready], 16)

            def load_xf(b, slot, ready):
                sp.dma_start(xf[:, slot].rearrange("p a k t -> p (a k t)"),
                             xf_dram[bass.ds(b, 1)].rearrange("a p c -> p (a c)")).then_inc(in_xf[ready], 16)

            def store_xf(n):
                sp.wait_ge(spread_lo[2], (n + 1) * KT)
                sp.dma_start(xf_dram[bass.ds(n, 1)].rearrange("a p c -> p (a c)"),
                             o_t[:].rearrange("p a k t -> p (a k t)")).then_inc(xf_stored, 16)

            def load_packed(nb):
                for i, src in enumerate((gate_p, up_p)):
                    rows = src.rearrange("(n p r) w -> n p r w", p=P, r=2)
                    sp.dma_start(pk_in[:, 2 * i:2 * i + 2, :], rows[bass.ds(nb, 1)].rearrange("a p r w -> p (a r) w")).then_inc(ld_pk, 16)
                cols = down_p.rearrange("(t p) (n w) -> n p t w", p=P, w=P)
                sp.dma_start(pk_in[:, 4:6, :].rearrange("p a (b w) -> p (a b) w", w=P),
                             cols[bass.ds(nb, 1)].rearrange("a p t w -> p (a t) w")).then_inc(ld_pk, 16)

            def body(n, last):
                first_nb = n * (NB // B)
                load_packed(first_nb)
                if not last:
                    load_ctx(n + 1)
                else:
                    sp.wait_ge(sd_stored, 16 * NB)
                    sp.wait_ge(v_out, B * TT)
                    load_half(0, 0, 0)
                    load_half(1, 1, 1)
                for r in range(NB // B):
                    nb = first_nb + r
                    if r + 1 < NB // B:
                        sp.wait_ge(pk_conv, 6 * nb + 6)
                        load_packed(nb + 1)
                    sp.wait_ge(pk_out0, nb + 1)
                    sp.dma_start(packed_t[bass.ds(2 * nb, 1)].rearrange("a p c -> p (a c)"), pk_t[:, 0]).then_inc(pk_stored, 16)
                    sp.wait_ge(pk_out1, nb + 1)
                    sp.dma_start(packed_t[bass.ds(2 * nb + 1, 1)].rearrange("a p c -> p (a c)"), pk_t[:, 1]).then_inc(pk_stored, 16)
                    if last and r == 1:
                        sp.wait_ge(dq_full, 1)
                        load_half(2, 0, 0)
                sp.wait_ge(pk_stored, 32 * (first_nb + NB // B))
                if not last:
                    stack_heads(n + 1, range(2 * HG))
                else:
                    sp.wait_ge(s_full, B * ROWS)
                    load_xf(0, 0, 0)
                    sp.wait_ge(dq_full, 2)
                    load_half(3, 1, 1)
                if not last:
                    store_xf(n)
            walk(body)(sp)

            def mlp_loads(i2, odd, dequant, nxt):
                it = 2 * i2 + odd
                if dequant:
                    sp.wait_ge(dq_full, it + 3)
                    load_half(it + 4, odd, odd)
                if nxt:
                    if not isinstance(it, int) or it > 0:
                        sp.wait_ge(down_done, 4 * it - 1 + 1)
                    load_xf((it + 1) % B, 1 - odd, 1 - odd)

            def store(it):
                sp.wait_ge(acc_out, it + 1)
                sp.dma_start(out[it % B].rearrange("(t p) d -> p t d", p=P), X[:, (it % B) * TT:(it % B + 1) * TT, :]).then_inc(out_stored, 16)

            mlp_loads(0, 0, True, True)
            store_xf(B - 1)
            sp.wait_ge(xf_stored, 16 * B + 16)
            mlp_loads(0, 1, True, True)
            with sp.Fori(1, 14) as i2:
                mlp_loads(i2, 0, True, True)
                mlp_loads(i2, 1, True, True)
            for it in range(28, 32):
                mlp_loads(it // 2, it % 2, False, it < 31)
                if it > 28:
                    store(it - 1)
            store(31)
            sp.wait_ge(out_stored, 16 * B)

        @block.gpsimd
        def _(pool):
            nc.gpsimd.memset(ones[:], 1.0).then_inc(const_ones, 1)
            pool.wait_ge(const_ones, 1)
            nc.gpsimd.affine_select(out=mask[:], in_=ones[:], compare_op=ALU.is_ge, fill=0.0, base=3 * P,
                                    pattern=[[-1, T]], channel_multiplier=1).then_inc(const_done, 1)
            nc.gpsimd.affine_select(out=ident[:], in_=ones[:, 0:P], compare_op=ALU.is_equal, fill=0.0, base=0,
                                    pattern=[[-1, P]], channel_multiplier=1).then_inc(const_done, 1)
            nc.gpsimd.affine_select(out=ident16[:], in_=ones[:, 0:P], compare_op=ALU.is_equal, fill=0.0, base=0,
                                    pattern=[[-1, P]], channel_multiplier=1).then_inc(const_done, 1)
            pool.wait_ge(most_done, 2)
            nc.gpsimd.partition_all_reduce(most_all[:, 0:2], most[:, 0:2], P, RMAX).then_inc(all_done, 1)
            pool.wait_ge(most_done, 7)
            nc.gpsimd.partition_all_reduce(most_all[:, 2:7], most[:, 2:7], P, RMAX).then_inc(all_done, 1)
            pool.wait_ge(fac_step, FAC_STEPS)
            pool.wait_ge(st_out, 17)
            for scales, factor in ((gu_st[1][0], C_SU[0:16]), (gu_st[1][1], C_SU[0:16]), (d_st[:], C_SD),
                                   (gu_st[0][0], C_SG[0:16]), (gu_st[0][1], C_SG[0:16])):
                nc.gpsimd.tensor_scalar(scales, scales, factor, None, ALU.mult).then_inc(st_scaled, 1)

            def dequant_part(hb, part):
                what, nib = part // 2, part % 2
                if part == 0:
                    pool.wait_ge(dq_step, hb * 6 + 6)
                    if hb > 0:
                        pool.wait_ge(dq_lo, hb)
                full, head, tail = w_full[:, nib], ring[:, hb, 0, nib], ring[:, hb, 1, nib]
                if what == 0:
                    ins, done = nc.gpsimd.tensor_tensor(full, codes[:, nib].bitcast(F16), sc_in[:, hb % 2], ALU.mult), dq_full
                elif what == 1:
                    pool.wait_ge(dq_full, hb + 1)
                    ins, done = nc.gpsimd.tensor_copy(head, full), dq_hi
                else:
                    pool.wait_ge(dq_hi, hb + 1)
                    ins, done = nc.gpsimd.tensor_tensor(tail, full, head, ALU.subtract), dq_lo
                if nib == 1:
                    ins.then_inc(done, 1)

            def convert(nb, r, a):
                if a == 0:
                    if r > 0:
                        pool.wait_ge(pk_full, 2 * nb)
                    alone(pool, ld_pk, (nb + 1) * 48)
                nc.gpsimd.tensor_copy(pk_16[:, a], pk_in[:, a].bitcast(U8).rearrange("p (c four) -> p c four", four=4)[:, :, 0]).then_inc(pk_conv, 1)

            def masked_values(n, u):
                hg, i = u // TT, u % TT
                if u >= 2:
                    pool.wait_ge(av_done, n * UNITS + u - 1)
                if u == 0:
                    pool.wait_ge(vb_out, n * (TT - 1) + TT - 1)
                pool.wait_ge(e_zero_done, beyond_units(n, u))
                nc.gpsimd.tensor_tensor(v_zero[:, u % 2].rearrange("p (j d) -> p j d", j=4),
                                        v_beyond[:, i, P * hg:P * hg + P].rearrange("p (j d) -> p j d", j=4),
                                        e_zero[:, u % 2, :].unsqueeze(2).to_broadcast([P, 4, DH]), ALU.mult).then_inc(v_zero_done, 1)

            def out_tail(n, hg):
                pool.wait_ge(o_hi, n * HG + hg + 1)
                nc.gpsimd.tensor_tensor(o_t[:, 1, hg, :], o_sum[:], o_t[:, 0, hg, :], ALU.subtract).then_inc(o_lo, 1)

            beside = {4: (0, 0), 5: (0, 1), 8: (0, 2), 9: (0, 3), 12: (0, 4), 13: (0, 5)}

            def body(n, last):
                for u in range(UNITS):
                    r, i = u // TT, u % TT
                    if i == 2 and r > 0:
                        out_tail(n, r - 1)
                    if i < TT - 1:
                        masked_values(n, u)
                    if i > 1:
                        for a in range(3 * i - 6, 3 * i - 3):
                            convert(n * (NB // B) + r, r, a)
                    if last and u in beside:
                        dequant_part(*beside[u])
                if last:
                    for hb in (1, 2, 3):
                        for part in (0, 1, 4, 5):
                            dequant_part(hb, part)

            walk(body)(pool)

        @block.tensor
        def _(pe):
            def three(o, lhs, rhs, first, stop):
                pe.matmul(o, lhs(0), rhs(0), start=first, stop=False)
                pe.matmul(o, lhs(0), rhs(1), start=False, stop=False)
                return pe.matmul(o, lhs(1), rhs(0), start=False, stop=stop)

            def spread(st, n, banks):
                for k in range(KT):
                    for t in range(TT):
                        if st < 2:
                            src = xn[:, t, P * k:P * k + P]
                        else:
                            src = xn[:, t, 256 * (k // 2) + k % 2:256 * (k // 2) + 256:2]
                        mm = pe.transpose(bank[banks + k][:, P * t:P * t + P], src, ident[:])
                    mm.then_inc(spread_full[st], 1)

            def qkv(n, groups):
                for g in groups:
                    bk = bank[g % 4]
                    if g == 0:
                        pe.wait_ge(spread_lo[0], n * KT + KT)
                    if isinstance(n, int) and n == 0 and g in (0, 1, 8):
                        pe.wait_ge(w_lo, 3 if g == 8 else g + 1)
                    if g >= 4:
                        pe.wait_ge(qk_lo, n * 8 + min(g - 3, 8))
                    for k in range(KT):
                        if g < 8:
                            w, c = g % 2, g // 2
                            mm = three(bk[:], lambda a: w_split[:, w, a, k, P * c:P * c + P], lambda a: xt[:, a, k, :], k == 0, k == KT - 1)
                        else:
                            t = g - 8
                            mm = three(bk[:], lambda a: xt[:, a, k, P * t:P * t + P], lambda a: w_split[:, 2, a, k, :], k == 0, k == KT - 1)
                    mm.then_inc(qkv_full, 1)

            def scores(n, u, j):
                hg, i = u // TT, u % TT
                if i == 0 and j == 0:
                    for g in (2 * hg, 2 * hg + 1):
                        pe.wait_ge(stacked[g % 4], n * 128 + 64 * (g // 4) + 64)
                if u > 0:
                    pe.wait_ge(exp_done, n * ROWS + 4 * (u - 1) + j + 1)
                elif j == 3:
                    pe.wait_ge(vb_out, n * (TT - 1) + TT - 1)
                h = 4 * hg + j
                pe.matmul(bank[j][:, 0:wide[i]], stack[:, 0, h, P * i:P * i + P], stack[:, 1, h, 0:wide[i]],
                          start=True, stop=True).then_inc(s_full, 1)

            def turn(n, u, j):
                i, slot = u % TT, turn_slot(4 * u + j)
                pe.wait_ge(exp_done, n * ROWS + 4 * u + j + 1)
                if slot < 3:
                    pe.wait_ge(att_lo, n * KT + (1, 2, 4)[slot])
                if slot >= 3:
                    pe.wait_ge(*turn_read(n, slot - 3))
                for k in range(wide[i] // P):
                    mm = pe.transpose(turn_bank(slot)[:, P * k:P * k + P], prob[:, u % 2, j, P * k:P * k + P], ident[:])
                mm.then_inc(t_full, 1)

            def values(n, u):
                hg, i = u // TT, u % TT
                pe.wait_ge(pt_act, n * 3 * UNITS + 3 * u + 3)
                pe.wait_ge(pt_dve, n * UNITS + u + 1)
                if u >= 1:
                    pe.wait_ge(o_done, n * UNITS + u)
                blocks = wide[i] // P
                at = P * (u % 2)
                if i < TT - 1:
                    pe.wait_ge(v_zero_done, beyond_units(n, u))
                for k in range(blocks + (i < TT - 1)):
                    for j in range(4):
                        h = 4 * hg + j
                        lhs, rhs = (V[:, k, DH * h:DH * h + DH], prob_t[:, u % 2, j, P * k:P * k + P]) if k < blocks else \
                                   (v_zero[:, u % 2, DH * j:DH * j + DH], ident[:])
                        mm = pe.matmul(bank[6][32 * j:32 * j + 32, at:at + P], lhs, rhs, start=(k == 0), stop=(k == blocks - (i == TT - 1)))
                mm.then_inc(av_done, 1)

            def recips(n, u):
                slot = recip_slot(u)
                pe.wait_ge(*turn_read(n, slot - 3))
                pe.wait_ge(rcol_done, n * UNITS + u + 1)
                for j in range(4):
                    mm = pe.matmul(turn_bank(slot)[32 * j:32 * j + 32, 0:P], r_col[:, u % 2, j:j + 1].to_broadcast([P, DH]), ident[:], start=True, stop=True)
                mm.then_inc(r_full, 1)

            def out_proj(n):
                pe.wait_ge(o_lo, n * HG + HG)
                pe.wait_ge(pk_out0, (n + 1) * (NB // B))
                pe.wait_ge(pk_out1, (n + 1) * (NB // B))
                for t in range(TT):
                    for k in range(KT):
                        mm = three(bank[4 + t][:], lambda a: o_t[:, a, k, P * t:P * t + P], lambda a: w_split[:, 3, a, k, :], k == 0, k == KT - 1)
                    mm.then_inc(wo_full, 1)

            def mix(n):
                pe.wait_ge(spread_lo[1], n * KT + KT)
                pe.wait_ge(att_lo, n * KT + KT)
                for t in range(TT):
                    for k in range(KT):
                        mm = three(bank[4 + t][:], lambda a: o_t[:, a, k, P * t:P * t + P], lambda a: att_t[:, a, k, :], k == 0, k == KT - 1)
                    mm.then_inc(mix_full, 1)

            def context_in(n):
                pe.wait_ge(ld_ctx, n * 16 + 16)
                for cc in range(2):
                    for t in range(TT):
                        mm = pe.transpose(bank[4 + cc][:, P * t:P * t + P], c_in[:, t, P * cc:P * cc + P], ident[:])
                    mm.then_inc(ct_full, 1)

            def context_qk(n):
                pe.wait_ge(ct_done, n * 2 + 2)
                for i in range(2):
                    for cc in range(2):
                        mm = pe.matmul(bank[6 + i][:], xw_t[:, cc, i, :], c_t[:, cc, :], start=(cc == 0), stop=(cc == 1))
                    mm.then_inc(qkx_full, 1)

            def value_sum(n, m):
                if m == 0:
                    pe.wait_ge(v_out, n * TT + TT)
                else:
                    pe.wait_ge(vb_out, n * (TT - 1) + m)
                pe.matmul(bank[3][:], mask[:, 0:P], V[:, TT - 1 - m, :], start=True, stop=True).then_inc(vb_full, 1)

            def energies(n):
                pe.wait_ge(qkx_done, n * 2 + 2)
                for m in range(TT):
                    pe.matmul(bank[4 + m][:], qk_x[:, 0, P * m:P * m + P], qk_x[:, 1, :], start=True, stop=True).then_inc(en_full, 1)

            def context_out(n, pieces):
                pe.wait_ge(en_step, n * 5 + 5)
                for k in pieces:
                    for m in range(TT):
                        mm = pe.transpose(bank[4 + k][:, P * m:P * m + P], e_p[:, m, P * k:P * k + P], ident[:])
                    mm.then_inc(att_full, 1)

            def repack(n, r):
                nb = n * (NB // B) + r
                pe.wait_ge(pk_conv, 6 * nb + 6)
                for half in range(2):
                    pe.wait_ge(*turn_read(n, pack_slot(r, half) - 3))
                    bk = turn_bank(pack_slot(r, half))[:].bitcast(F16)
                    tiles = [[(0, 0), (1, 0)], [(0, 1), (1, 1)], [(2, 0), (3, 0)]] if half == 0 else \
                            [[(2, 1), (3, 1)], [(4, 0), (4, 1)], [(5, 0), (5, 1)]]
                    for q in range(3):
                        for e, (a, w) in enumerate(tiles[q]):
                            mm = pe.transpose(bk[:, 256 * q + P * e:256 * q + P * e + P], pk_16[:, a, P * w:P * w + P], ident16[:])
                    mm.then_inc(pk_full, 1)

            def gate_up(it, par, s):
                g4 = 4 * ((it // 4) % 2)
                nbl, r = s // 2, s % 2
                if s == 0:
                    pe.wait_ge(in_xf[par], 16 * (it // 2) + 16)
                if s % 2 == 0:
                    pe.wait_ge(dq_lo, 4 * (it // 4) + 2 * nbl + 2)
                for which in range(2):
                    done = (g_full, u_full)[which]
                    bk = bank[2 * (s % 2) + which]
                    if not (isinstance(it, int) and it == 0 and s < 2):
                        pe.wait_ge((sq_out, int_out)[which], 4 * it + s - 1)
                    for k in range(KT):
                        kk, nib = k // 2, k % 2
                        if which == 0:
                            off, at = 0, 256 * kk
                        else:
                            off, at = (0, 512) if kk == 0 else (1, 0)
                        slot = g4 + 2 * nbl + off

                        def w(a):
                            if isinstance(slot, int):
                                return ring[:, slot, a, nib, at + P * r:at + P * r + P]
                            return ring[:, bass.ds(slot, 1), a, nib, at + P * r:at + P * r + P].rearrange("p a c -> p (a c)")
                        mm = three(bk[:], w, lambda a: xf[:, par, a, k, :], k == 0, k == KT - 1)
                    mm.then_inc(done, 1)

            def down(it, par, s):
                g4 = 4 * ((it // 4) % 2)
                nbl, r = s // 2, s % 2
                pe.wait_ge(hid_lo, 4 * it + s + 1)
                if s == 0 and not (isinstance(it, int) and it == 0):
                    pe.wait_ge(acc_out, it)
                slot = g4 + 2 * nbl + 1

                def w(a):
                    if isinstance(slot, int):
                        return ring[:, slot, a, r, 256:768]
                    return ring[:, bass.ds(slot, 1), a, r, 256:768].rearrange("p a c -> p (a c)")
                for t in range(TT):
                    mm = three(bank[4 + t][:], lambda a: hid[:, s % 2, a, P * t:P * t + P], w, s == 0, s == 3)
                mm.then_inc(down_done, 1)

            def iteration(it, par, nxt, begun=1):
                for s in range(4):
                    if s + 1 < begun:
                        pass
                    elif s < 3:
                        gate_up(it, par, s + 1)
                    elif nxt:
                        gate_up(it + 1, 1 - par, 0)
                    down(it, par, s)

            def turn_scales():
                for g in range(17):
                    if g >= 4:
                        pe.wait_ge(st_out, g - 3)
                    for e in range(4):
                        o = bank[4 + g % 4][0:16, P * e:P * e + P] if g < 16 else bank[4][:, P * e:P * e + P]
                        mm = pe.transpose(o, gs_in[:, g // 8, 4 * (g % 8) + e, :] if g < 16 else ds_in[:, e, :], ident[:])
                    mm.then_inc(st_full, 1)

            def turn_context_weights():
                pe.wait_ge(ld_small, 64)
                pe.wait_ge(st_out, 17)
                for cc in range(2):
                    for i in range(2):
                        mm = pe.transpose(bank[5][:, 256 * cc + P * i:256 * cc + P * i + P], xw[:, i, P * cc:P * cc + P], ident[:])
                mm.then_inc(xw_full, 1)

            def between(n, prev, nxt):
                if nxt:
                    qkv(n + 1, (0, 1))
                if prev:
                    out_proj(n)
                if nxt:
                    qkv(n + 1, (2, 3, 4, 5))
                else:
                    gate_up(0, 0, 0)
                    gate_up(0, 0, 1)
                if prev:
                    pe.wait_ge(ln_done[1], (n + 1) * TT)
                    spread(1, n, 4)
                if nxt:
                    qkv(n + 1, (6,))
                else:
                    gate_up(0, 0, 2)
                if prev:
                    mix(n)
                if nxt:
                    qkv(n + 1, (7,))
                    if prev:
                        pe.wait_ge(x2_done, n * TT + TT)
                    else:
                        pe.wait_ge(xw_done, 1)
                        pe.wait_ge(w_lo, 4)
                    context_in(n + 1)
                    qkv(n + 1, (8,))
                    context_qk(n + 1)
                    qkv(n + 1, (9,))
                    energies(n + 1)
                    qkv(n + 1, (10,))
                if prev and nxt:
                    pe.wait_ge(ln_done[2], (n + 1) * TT)
                    pe.wait_ge(en_exp, (n + 2) * TT)
                    spread(2, n, 4)
                if nxt:
                    qkv(n + 1, (11,))
                    value_sum(n + 1, 0)
                    for j in range(AHEAD):
                        scores(n + 1, 0, j)
                    if prev:
                        pe.wait_ge(spread_lo[2], (n + 1) * KT)
                    context_out(n + 1, (0, 1))
                    value_sum(n + 1, 1)
                    context_out(n + 1, (2, 3))
                    value_sum(n + 1, 2)

            pe.wait_ge(const_done, 3)
            pe.wait_ge(ld_s, 48)
            turn_scales()
            pe.wait_ge(ln_done[0], TT)
            spread(0, 0, 0)
            turn_context_weights()
            between(-1, False, True)

            def body(n, last):
                for j in range(AHEAD, 4):
                    scores(n, 0, j)
                for u in range(UNITS):
                    for j in range(4):
                        if u + 1 < UNITS:
                            scores(n, u + 1, j)
                        turn(n, u, j)
                        if j == 3 and u > 0:
                            recips(n, u - 1)
                            values(n, u - 1)
                        if j == 1 and u % TT == 0 and u > 0:
                            repack(n, u // TT - 1)
                repack(n, HG - 1)
                recips(n, UNITS - 1)
                if not last:
                    pe.wait_ge(ln_done[0], (n + 2) * TT)
                    pe.wait_ge(exp_done, (n + 1) * ROWS)
                    spread(0, n + 1, 0)
                values(n, UNITS - 1)
                between(n, True, not last)

            walk(body)(pe)

            pe.wait_ge(x2_done, B * TT)
            iteration(0, 0, True, begun=3)
            gate_up(1, 1, 1)
            pe.wait_ge(ln_done[2], B * TT)
            pe.wait_ge(acc_out, 1)
            spread(2, B - 1, 4)
            pe.wait_ge(spread_lo[2], B * KT)
            iteration(1, 1, True, begun=2)
            with pe.Fori(1, 15) as i2:
                iteration(2 * i2, 0, True)
                iteration(2 * i2 + 1, 1, True)
            iteration(30, 0, True)
            iteration(31, 1, False)

        @block.scalar
        def _(act):
            def spread_heads(st, n, banks):
                dst = xt if st == 0 else o_t
                for k in range(KT):
                    act.wait_ge(spread_full[st], n * KT + k + 1)
                    nc.scalar.activation(dst[:, 0, k, :], bank[banks + k][:], ACT.Copy, scale=XS).then_inc(spread_hi[st], 1)

            def qkv_heads(n, groups):
                for g in groups:
                    act.wait_ge(qkv_full, n * 12 + g + 1)
                    if g < 8:
                        if g >= 4:
                            act.wait_ge(qk_in[g % 4], n * 32 + 16)
                        elif not isinstance(n, int) or n > 0:
                            act.wait_ge(qk_in[g % 4], n * 32)
                        nc.scalar.activation(qk[:, g % 4, 0, :], bank[g % 4][:], ACT.Copy, scale=QS).then_inc(qk_hi, 1)
                    else:
                        nc.scalar.copy(V[:, g - 8, :], bank[g % 4][:]).then_inc(v_out, 1)

            def exp(n, u, j):
                i = u % TT
                act.wait_ge(shift_done, n * ROWS + 4 * u + j + 1)
                if u >= 2:
                    act.wait_ge(t_full, n * ROWS + 4 * (u - 2) + j + 1)
                nc.scalar.activation(prob[:, u % 2, j, 0:wide[i]], bank[j][:, 0:wide[i]], ACT.Exp,
                                     bias=nmx[:, u % 2, j:j + 1], accum_out=den[:, u % 2, j:j + 1]).then_inc(exp_done, 1)

            def exp_zero(n, u):
                if u >= 2:
                    act.wait_ge(den_done, beyond_units(n, u - 2))
                    act.wait_ge(v_zero_done, beyond_units(n, u - 2))
                act.wait_ge(shift_done, n * ROWS + 4 * u + 4)
                nc.scalar.activation(e_zero[:, u % 2, :], nmx[:, u % 2, :], ACT.Exp).then_inc(e_zero_done, 1)

            def turned(n, u, j):
                i = u % TT
                act.wait_ge(t_full, n * ROWS + 4 * u + j + 1)
                if u >= 2:
                    act.wait_ge(av_done, n * UNITS + u - 1)
                nc.scalar.copy(prob_t[:, u % 2, j, 0:wide[i]], turn_bank(turn_slot(4 * u + j))[:, 0:wide[i]]).then_inc(pt_act, 1)

            def recip_out(n, u):
                act.wait_ge(r_full, n * UNITS + u + 1)
                if u >= 2:
                    act.wait_ge(o_done, n * UNITS + u - 1)
                nc.scalar.copy(r_den[:, u % 2, :], turn_bank(recip_slot(u))[:, 0:P]).then_inc(rden_out, 1)

            def out_head(n, hg):
                act.wait_ge(o_done, n * UNITS + 4 * hg + 4)
                if hg == 0:
                    act.wait_ge(xf_stored, n * 16 + 16)
                nc.scalar.copy(o_t[:, 0, hg, :], o_sum[:]).then_inc(o_hi, 1)

            def repacked(n, r):
                nb = n * (NB // B) + r
                act.wait_ge(pk_full, 2 * nb + 1)
                if r > 0:
                    act.wait_ge(pk_stored, 32 * nb)
                nc.scalar.copy(pk_t[:, 0], turn_bank(pack_slot(r, 0))[:].bitcast(F16)[:, 0:HALF]).then_inc(pk_out0, 1)

            def context_in(n):
                for cc in range(2):
                    act.wait_ge(ct_full, n * 2 + cc + 1)
                    nc.scalar.copy(c_t[:, cc, :], bank[4 + cc][:]).then_inc(ct_done, 1)

            def context_qk(n):
                for i in range(2):
                    act.wait_ge(qkx_full, n * 2 + i + 1)
                    nc.scalar.activation(qk_x[:, i, :], bank[6 + i][:], ACT.Identity, bias=xb[:, i:i + 1]).then_inc(qkx_done, 1)

            def energy_exp(n):
                for m in range(TT):
                    act.wait_ge(en_max, n * TT + m + 1)
                    nc.scalar.activation(e_p[:, m, :], bank[4 + m][:], ACT.Exp, bias=x_nm[:, m:m + 1],
                                         accum_out=x_den[:, m:m + 1]).then_inc(en_exp, 1)

            def value_sum_out(n):
                if isinstance(n, int) and n == 0:
                    act.wait_ge(su_stored, 16 * 4)
                act.wait_ge(vb_full, n * (TT - 1) + 1)
                nc.scalar.copy(v_beyond[:, TT - 2, :], bank[3][:]).then_inc(vb_out, 1)

            def context_heads(n):
                for k in range(KT):
                    act.wait_ge(att_full, n * KT + k + 1)
                    nc.scalar.copy(att_t[:, 0, k, :], bank[4 + k][:]).then_inc(att_hi, 1)

            def dequant(hb, slot):
                act.wait_ge(dq_full, hb + 1)
                nc.scalar.copy(ring[:, slot, 0] if isinstance(slot, int) else ring[:, bass.ds(slot, 1), 0].rearrange("p a b c -> p (a b) c"),
                               w_full[:]).then_inc(dq_hi, 1)

            def gate(it, s):
                q = s % 2
                step = 4 * it + s
                early = isinstance(it, int) and it == 0 and s < 2
                act.wait_ge(g_full, step + 1)
                if not early:
                    act.wait_ge(gel_out, step - 1)
                nc.scalar.activation(g_sb[:, q], bank[2 * q][:], ACT.Copy, scale=C_G)
                if not early:
                    act.wait_ge(cube_out, step - 1)
                nc.scalar.activation(sq[:, q], bank[2 * q][:], ACT.Square, scale=C_G).then_inc(sq_out, 1)
                act.wait_ge(cube_out, step + 1)
                nc.scalar.activation(th[:, q], cube[:, q], ACT.Tanh, scale=GELU_A * GELU_B).then_inc(th_out, 1)
                act.wait_ge(int_out, step + 1)
                if not early:
                    act.wait_ge(down_done, step - 1)
                nc.scalar.copy(hid[:, q, 0], inter[:, q]).then_inc(hid_hi, 1)

            def between(n, prev, nxt):
                if nxt:
                    qkv_heads(n + 1, (0, 1))
                    if not prev:
                        act.wait_ge(fac_step, 6 + 4)
                        split_heads((2, 3))
                    qkv_heads(n + 1, (2, 3, 4, 5))
                else:
                    for hb in (1, 2, 3):
                        dequant(hb, hb)
                    gate(0, 0)
                if prev:
                    spread_heads(1, n, 4)
                if nxt:
                    qkv_heads(n + 1, (6, 7))
                    context_in(n + 1)
                    qkv_heads(n + 1, (8,))
                    context_qk(n + 1)
                    qkv_heads(n + 1, (9,))
                    energy_exp(n + 1)
                    qkv_heads(n + 1, (10,))
                if prev and nxt:
                    spread_heads(2, n, 4)
                if nxt:
                    qkv_heads(n + 1, (11,))
                    value_sum_out(n + 1)
                    for j in range(AHEAD):
                        exp(n + 1, 0, j)
                    context_heads(n + 1)

            def split_heads(which):
                for w in which:
                    nc.scalar.activation(w_split[:, w, 0], w_raw[:, w], ACT.Copy, scale=fac[:, w:w + 1]).then_inc(w_hi, 1)

            for g in range(17):
                act.wait_ge(st_full, g + 1)
                dst, src = (gu_st[g // 8][g % 8 // 4][:, 512 * (g % 4):512 * (g % 4) + 512], bank[4 + g % 4][0:16, :]) if g < 16 else (d_st[:], bank[4][:])
                nc.scalar.copy(dst, src).then_inc(st_out, 1)

            spread_heads(0, 0, 0)
            act.wait_ge(xw_full, 1)
            nc.scalar.copy(xw_t[:].rearrange("p a b c -> p (a b c)"), bank[5][:]).then_inc(xw_done, 1)
            act.wait_ge(fac_step, 4)
            split_heads((0, 1))
            act.wait_ge(ld_small, 64)
            between(-1, False, True)

            def body(n, last):
                for u in range(UNITS):
                    for j in range(4):
                        if u == 1 and j == 0:
                            act.wait_ge(att_full, n * KT + KT)
                        if u > 0 or j >= AHEAD:
                            exp(n, u, j)
                        if j == 3 and u % TT < TT - 1:
                            exp_zero(n, u)
                        if j == AT_OUT and u % TT == 2 and u > TT:
                            out_head(n, u // TT - 1)
                        if j >= 2:
                            turned(n, u, j - 2)
                        elif j == 0 and u > 0:
                            turned(n, u - 1, 2)
                        if j == 3 and u % TT == 0 and u > 0:
                            repacked(n, u // TT - 1)
                        h = 4 * u + j - AT_RECIP
                        if h >= 0 and h % 4 == 0:
                            recip_out(n, h // 4)
                turned(n, UNITS - 1, 2)
                for u in range((ROWS - 1 - AT_RECIP) // 4 + 1, UNITS - 1):
                    recip_out(n, u)
                repacked(n, HG - 1)
                recip_out(n, UNITS - 1)
                if not last:
                    spread_heads(0, n + 1, 0)
                out_head(n, HG - 1)
                between(n, True, not last)

            walk(body)(act)

            def iteration(it, deq, nxt):
                for s in range(4):
                    if s < 3:
                        gate(it, s + 1)
                    elif nxt:
                        gate(it + 1, 0)
                    if s == 0 and deq:
                        if not isinstance(it, int) or it > 0:
                            act.wait_ge(down_done, 4 * it)
                        dequant(it + 4, (it + 4) % 8)

            for s in range(1, 4):
                gate(0, s)
            gate(1, 0)
            spread_heads(2, B - 1, 4)
            gate(1, 1)
            dequant(4, 4)
            gate(1, 2)
            gate(1, 3)
            gate(2, 0)
            dequant(5, 5)
            with act.Fori(2, 28) as it:
                iteration(it, True, True)
            with act.Fori(28, 31) as it:
                iteration(it, False, True)
            iteration(31, False, False)

        @block.vector
        def _(dve):
            def norm_part(st, n, part):
                tile = lambda t: X[:, t, :] if isinstance(t, int) else X[:, bass.ds(t, 1), :].rearrange("p a d -> p (a d)")
                t = part % TT
                if part == TT:
                    alone(dve, ln_step[st], n * (LN_PARTS - TT) + part)
                elif 2 * TT <= part <= LN_PARTS - TT:
                    dve.wait_ge(ln_step[st], n * (LN_PARTS - TT) + part)
                if part < TT:
                    ins = nc.vector.bn_stats(st6[:, t, :], tile(n * TT + t))
                elif part < 2 * TT:
                    ins = nc.vector.bn_aggr(mv[:, t, :], st6[:, t, :])
                elif part == 2 * TT:
                    ins = nc.vector.tensor_scalar(var[:], mv[:, :, 1], EPS, None, ALU.add)
                elif part == 2 * TT + 1:
                    ins = nc.vector.tensor_scalar(rsi[:], var[:].bitcast(I32), 1, None, ALU.logical_shift_right)
                elif part == 2 * TT + 2:
                    ins = nc.vector.tensor_scalar(rs[:, 0].bitcast(I32), rsi[:], -1.0, float(0x5F3759DF), ALU.mult, ALU.add)
                elif part < LN_PARTS - TT:
                    newton = (part - 2 * TT) % 3
                    if newton == 0:
                        ins = nc.vector.tensor_tensor(rs[:, 1], rs[:, 0], rs[:, 0], ALU.mult)
                    elif newton == 1:
                        ins = nc.vector.scalar_tensor_tensor(rs[:, 1], rs[:, 1], -0.5, var[:], ALU.mult, ALU.mult)
                    else:
                        ins = nc.vector.scalar_tensor_tensor(rs[:, 0], rs[:, 1], 1.5, rs[:, 0], ALU.add, ALU.mult)
                else:
                    t = part - (LN_PARTS - TT)
                    nc.vector.tensor_scalar(xn[:, t, :], tile(n * TT + t), mv[:, t, 0:1], rs[:, 0, t:t + 1],
                                            ALU.subtract, ALU.mult).then_inc(ln_done[st], 1)
                    return
                ins.then_inc(ln_step[st], 1)

            def norm(st, n):
                for part in range(LN_PARTS):
                    norm_part(st, n, part)

            def spread_tails(st, n, banks):
                dst = xt if st == 0 else o_t
                for k in range(KT):
                    dve.wait_ge(spread_hi[st], n * KT + k + 1)
                    nc.vector.scalar_tensor_tensor(dst[:, 1, k, :], bank[banks + k][:], XS, dst[:, 0, k, :],
                                                   ALU.mult, ALU.subtract).then_inc(spread_lo[st], 1)

            def qkv_tails(n, groups):
                for g in groups:
                    dve.wait_ge(qk_hi, n * 8 + g + 1)
                    nc.vector.scalar_tensor_tensor(qk[:, g % 4, 1, :], bank[g % 4][:], QS, qk[:, g % 4, 0, :],
                                                   ALU.mult, ALU.subtract).then_inc(qk_lo, 1)

            def row_max(n, u, j):
                i = u % TT
                alone(dve, s_full, n * ROWS + 4 * u + j + 1)
                nc.vector.tensor_tensor_reduce(out=bank[j][:, 0:wide[i]], in0=bank[j][:, 0:wide[i]],
                                               in1=mask[:, P * (3 - i):P * (3 - i) + wide[i]], scale=C_EXP,
                                               scalar=0.0 if i < TT - 1 else NEG, op0=ALU.mult, op1=ALU.max,
                                               accum_out=mx[:, u % 2, j:j + 1]).then_inc(max_done, 1)

            def shift(n, u, j):
                dve.wait_ge(max_done, n * ROWS + 4 * u + j + 1)
                nc.vector.tensor_scalar(nmx[:, u % 2, j:j + 1], mx[:, u % 2, j:j + 1], -1.0, None, ALU.mult).then_inc(shift_done, 1)

            def turned(n, u):
                i = u % TT
                dve.wait_ge(t_full, n * ROWS + 4 * u + 4)
                if u >= 2:
                    dve.wait_ge(av_done, n * UNITS + u - 1)
                nc.vector.tensor_copy(prob_t[:, u % 2, 3, 0:wide[i]], turn_bank(turn_slot(4 * u + 3))[:, 0:wide[i]]).then_inc(pt_dve, 1)

            def all_tokens(n, u):
                i = u % TT
                if i < TT - 1:
                    dve.wait_ge(exp_done, n * ROWS + 4 * u + 4)
                    dve.wait_ge(e_zero_done, beyond_units(n, u))
                    nc.vector.scalar_tensor_tensor(den_all[:, u % 2, :], e_zero[:, u % 2, :], float(T - wide[i]), den[:, u % 2, :],
                                                   ALU.mult, ALU.add).then_inc(den_done, 1)

            def reciprocals(n, u):
                if u % TT < TT - 1:
                    dve.wait_ge(den_done, beyond_units(n, u))
                    sums = den_all
                else:
                    dve.wait_ge(exp_done, n * ROWS + 4 * u + 4)
                    sums = den
                nc.vector.reciprocal(r_col[:, u % 2, :], sums[:, u % 2, :]).then_inc(rcol_done, 1)

            def divide(n, u):
                hg, i = u // TT, u % TT
                if i == 0 and hg > 0:
                    dve.wait_ge(o_hi, n * HG + hg)
                    dve.wait_ge(o_lo, n * HG + hg)
                dve.wait_ge(rden_out, n * UNITS + u + 1)
                dve.wait_ge(av_done, n * UNITS + u + 1)
                nc.vector.scalar_tensor_tensor(o_sum[:, P * i:P * i + P], bank[6][:, P * (u % 2):P * (u % 2) + P], QS, r_den[:, u % 2, :],
                                               ALU.mult, ALU.mult).then_inc(o_done, 1)

            def out_tail(n, hg):
                dve.wait_ge(o_hi, n * HG + hg + 1)
                nc.vector.tensor_tensor(o_t[:, 1, hg, :], o_sum[:], o_t[:, 0, hg, :], ALU.subtract).then_inc(o_lo, 1)

            def repacked(n, r):
                nb = n * (NB // B) + r
                dve.wait_ge(pk_full, 2 * nb + 2)
                if r > 0:
                    dve.wait_ge(pk_stored, 32 * nb)
                nc.vector.tensor_copy(pk_t[:, 1], turn_bank(pack_slot(r, 1))[:].bitcast(F16)[:, 0:HALF]).then_inc(pk_out1, 1)

            def residual(n, full, banks, factor, done):
                for t in range(TT):
                    dve.wait_ge(full, n * TT + t + 1)
                    at = n * TT + t
                    xv = X[:, at, :] if isinstance(at, int) else X[:, bass.ds(at, 1), :].rearrange("p a d -> p (a d)")
                    nc.vector.scalar_tensor_tensor(xv, bank[banks + t][:], factor, xv, ALU.mult, ALU.add).then_inc(done, 1)
                alone(dve, done, n * TT + TT)

            def context(n):
                for m in range(TT):
                    dve.wait_ge(en_full, n * TT + m + 1)
                    nc.vector.tensor_reduce(x_nm[:, m:m + 1], bank[4 + m][:], AX.X, ALU.max, negate=True).then_inc(en_max, 1)
                dve.wait_ge(en_exp, n * TT + TT)
                nc.vector.reciprocal(x_rden[:], x_den[:]).then_inc(en_step, 1)
                dve.wait_ge(en_step, n * 5 + 1)
                for m in range(TT):
                    nc.vector.tensor_scalar(e_p[:, m, :], e_p[:, m, :], x_rden[:, m:m + 1], AS, ALU.mult, ALU.mult).then_inc(en_step, 1)

            def value_sum_out(n, m):
                if m == TT - 2 and isinstance(n, int) and n == 0:
                    dve.wait_ge(sd_stored, 16 * NB)
                dve.wait_ge(vb_full, n * (TT - 1) + m + 1)
                dve.wait_ge(vb_out, n * (TT - 1) + m)
                nc.vector.tensor_tensor(v_beyond[:, TT - 2 - m, :], bank[3][:], v_beyond[:, TT - 1 - m, :], ALU.add).then_inc(vb_out, 1)

            def context_tails(n, pieces):
                for k in pieces:
                    dve.wait_ge(att_hi, n * KT + k + 1)
                    nc.vector.tensor_tensor(att_t[:, 1, k, :], bank[4 + k][:], att_t[:, 0, k, :], ALU.subtract).then_inc(att_lo, 1)

            def unpack_part(hb, par, part):
                nib, what = part // 3, part % 3
                words = pk_in2[:, par].bitcast(U32)
                if part == 0:
                    dve.wait_ge(in_pk[par], 32 * (hb // 2) + 32)
                    if isinstance(hb, int) and 0 < hb < 4:
                        dve.wait_ge(dq_full, hb)
                if what != 1 and part > 0:
                    dve.wait_ge(dq_step, hb * 6 + part)
                if what == 0:
                    ins = nc.vector.tensor_scalar(bits[:], words, 9 - 4 * nib, 0x0E000E00, ALU.logical_shift_left, ALU.bitwise_and)
                elif what == 1:
                    ins = nc.vector.tensor_scalar(codes[:, nib], words, 12 - 4 * nib, 0x80008000, ALU.logical_shift_left, ALU.bitwise_and)
                else:
                    ins = nc.vector.tensor_tensor(codes[:, nib], codes[:, nib], bits[:], ALU.bitwise_or)
                ins.then_inc(dq_step, 1)

            def dequant(hb, slot, par):
                for part in range(6):
                    unpack_part(hb, par, part)
                dve.wait_ge(dq_step, hb * 6 + 6)
                if not isinstance(hb, int) or hb > 0:
                    dve.wait_ge(dq_lo, hb)
                sc = sc_in[:, par]
                nc.vector.tensor_tensor(w_full[:], codes[:].rearrange("p a c -> p (a c)").bitcast(F16).rearrange("p (a c) -> p a c", a=2),
                                        sc.unsqueeze(1).to_broadcast([P, 2, HALF]), ALU.mult).then_inc(dq_full, 1)
                dve.wait_ge(dq_hi, hb + 1)
                lo, hi = (ring[:, slot, a] if isinstance(slot, int) else ring[:, bass.ds(slot, 1), a].rearrange("p a b c -> p (a b) c") for a in (1, 0))
                nc.vector.tensor_tensor(lo, w_full[:], hi, ALU.subtract).then_inc(dq_lo, 1)

            def gate(it, s):
                q = s % 2
                step = 4 * it + s
                early = isinstance(it, int) and it == 0 and s < 2
                dve.wait_ge(sq_out, step + 1)
                if not early:
                    dve.wait_ge(th_out, step - 1)
                nc.vector.scalar_tensor_tensor(cube[:, q], sq[:, q], 1.0 / GELU_B, g_sb[:, q], ALU.add, ALU.mult).then_inc(cube_out, 1)
                dve.wait_ge(th_out, step + 1)
                nc.vector.scalar_tensor_tensor(gel[:, q], th[:, q], 1.0, g_sb[:, q], ALU.add, ALU.mult).then_inc(gel_out, 1)
                dve.wait_ge(gel_out, step + 1)
                dve.wait_ge(u_full, step + 1)
                nc.vector.scalar_tensor_tensor(inter[:, q], bank[2 * q + 1][:], C_I, gel[:, q], ALU.mult, ALU.mult).then_inc(int_out, 1)
                dve.wait_ge(hid_hi, step + 1)
                nc.vector.tensor_tensor(hid[:, q, 1], inter[:, q], hid[:, q, 0], ALU.subtract).then_inc(hid_lo, 1)

            def between(n, prev, nxt):
                if nxt:
                    qkv_tails(n + 1, (0, 1))
                if not prev:
                    split_tails((2, 3))
                if prev:
                    if not nxt:
                        for part in range(6):
                            unpack_part(2, 0, part)
                    residual(n, wo_full, 4, C_O, x1_done)
                    if not nxt:
                        for part in range(6):
                            unpack_part(3, 1, part)
                    norm(1, n)
                if nxt:
                    qkv_tails(n + 1, (2, 3, 4, 5))
                else:
                    gate(0, 0)
                if prev:
                    spread_tails(1, n, 4)
                if nxt:
                    qkv_tails(n + 1, (6,))
                else:
                    gate(0, 1)
                if prev:
                    residual(n, mix_full, 4, 1.0 / (XS * AS), x2_done)
                if prev and nxt:
                    norm(2, n)
                if nxt:
                    qkv_tails(n + 1, (7,))
                    context(n + 1)
                if prev and nxt:
                    spread_tails(2, n, 4)
                if nxt:
                    for j in range(AHEAD):
                        row_max(n + 1, 0, j)
                        shift(n + 1, 0, j)
                    context_tails(n + 1, (0, 1))
                    value_sum_out(n + 1, 1)
                    context_tails(n + 1, (2, 3))
                    value_sum_out(n + 1, 2)

            def largest(w):
                dve.wait_ge(ld_w[w], 16)
                nc.vector.tensor_reduce(most[:, w:w + 1], w_raw[:, w].rearrange("p k n -> p (k n)"), AX.X, ALU.max,
                                        apply_absolute_value=True).then_inc(most_done, 1)

            def factors(cols, reduced):
                e0, e1 = expo[:, 0, cols], expo[:, 1, cols]
                dve.wait_ge(all_done, reduced)
                steps.mark(nc.vector.tensor_scalar(e0, most_all[:, cols].bitcast(I32), 23, None, ALU.logical_shift_right))
                steps.settle()
                steps.mark(nc.vector.tensor_scalar(e1, e0, -1.0, float(TOP + 127), ALU.mult, ALU.add))
                steps.settle()
                steps.mark(nc.vector.tensor_scalar(e0, e1, float(CAP), None, ALU.min))
                steps.settle()
                steps.mark(nc.vector.tensor_scalar(fac[:, cols].bitcast(I32), e0, 23, None, ALU.logical_shift_left))
                steps.mark(nc.vector.tensor_scalar(e1, e0, -1.0, 254.0, ALU.mult, ALU.add))
                steps.settle()
                steps.mark(nc.vector.tensor_scalar(ifac[:, cols].bitcast(I32), e1, 23, None, ALU.logical_shift_left))
                steps.settle()

            def split_tails(which):
                for w in which:
                    dve.wait_ge(w_hi, w + 1)
                    nc.vector.scalar_tensor_tensor(w_split[:, w, 1], w_raw[:, w], fac[:, w:w + 1], w_split[:, w, 0],
                                                   ALU.mult, ALU.subtract).then_inc(w_lo, 1)

            dve.wait_ge(ld_x0, 16)
            norm(0, 0)
            for w in range(3):
                largest(w)
            steps = Steps(dve, fac_step, 0, FAC_STEPS)
            factors(slice(0, 2), 1)
            spread_tails(0, 0, 0)
            split_tails((0,))
            largest(3)
            dve.wait_ge(ld_s, 48)
            for i, scales in enumerate((gs_in[:, 0].rearrange("p n k -> p (n k)"), gs_in[:, 1].rearrange("p n k -> p (n k)"),
                                        ds_in[:].rearrange("p t k -> p (t k)"))):
                nc.vector.tensor_reduce(most[:, SG + i:SG + i + 1], scales, AX.X, ALU.max, apply_absolute_value=True).then_inc(most_done, 1)
            split_tails((1,))
            factors(slice(2, 7), 2)

            def pair(dst, a, s, b):
                steps.mark(nc.vector.scalar_tensor_tensor(dst, a, s, b, ALU.mult, ALU.mult))

            def one(dst, a, s):
                steps.mark(nc.vector.tensor_scalar(dst, a, s, None, ALU.mult))

            f = lambda i: fac[:, i:i + 1]
            r = lambda i: ifac[:, i:i + 1]
            pair(C_EXP, r(0), 2.0 ** 14 / float(np.sqrt(T)), r(1))
            pair(C_O, r(2), 2.0 ** 7, r(3))
            one(C_G, r(SG), 1.0 / XS)
            one(C_I, f(SG), 2.0 ** -46)
            pair(tmpc[:, 0:1], r(SG), 2.0 ** 34, r(SU))
            one(C_SG, f(SG), LUT)
            one(C_SU, f(SU), LUT)
            one(C_SD, f(SD), LUT)
            steps.settle()
            steps.mark(nc.vector.tensor_tensor(C_OUT, tmpc[:, 0:1], r(SD), ALU.mult))
            steps.settle()
            steps.end()
            between(-1, False, True)
            dve.wait_ge(ld_x1, 16)

            def body(n, last):
                for u in range(UNITS):
                    for j in range(4):
                        if u > 0 or j >= AHEAD:
                            row_max(n, u, j)
                        if j == AT_SUMS and u > 0:
                            all_tokens(n, u - 1)
                        if j == AT_TURNED and u > 0:
                            turned(n, u - 1)
                        if j == AT_RECIPROCALS and u > 0:
                            reciprocals(n, u - 1)
                        h = 4 * u + j - AT_DIVIDE
                        if h >= 0 and h % 4 == 0:
                            divide(n, h // 4)
                        if u > 0 or j >= AHEAD:
                            shift(n, u, j)
                        if j == 0 and u % TT == 1 and u > TT:
                            repacked(n, u // TT - 1)
                        hg, h = u // TT, (4 * u + j) % 16
                        if last and (hg, h // 6) in ((0, 1), (2, 0)):
                            unpack_part(hg // 2, hg // 2, h % 6)
                        part = (4 * u + j) // 2 - 2
                        if not last and j % 2 == 1 and 0 <= part < LN_PARTS:
                            norm_part(0, n + 1, part)
                all_tokens(n, UNITS - 1)
                reciprocals(n, UNITS - 1)
                turned(n, UNITS - 1)
                for u in range((ROWS - 1 - AT_DIVIDE) // 4 + 1, UNITS - 1):
                    divide(n, u)
                repacked(n, HG - 1)
                if not last:
                    spread_tails(0, n + 1, 0)
                divide(n, UNITS - 1)
                out_tail(n, HG - 1)
                between(n, True, not last)
                if not last:
                    dve.wait_ge(ld_x, 16 * (B - 2))

            walk(body)(dve)

            def add_out(it):
                dve.wait_ge(down_done, 4 * it + 4)
                for t in range(TT):
                    at = (it % B) * TT + t
                    xv = X[:, at, :] if isinstance(at, int) else X[:, bass.ds(at, 1), :].rearrange("p a d -> p (a d)")
                    ins = nc.vector.scalar_tensor_tensor(xv, bank[4 + t][:], C_OUT, xv, ALU.mult, ALU.add)
                ins.then_inc(acc_out, 1)

            def iteration(it, par, deq, nxt):
                for s in range(4):
                    if s < 3:
                        gate(it, s + 1)
                    elif nxt:
                        gate(it + 1, 0)
                    if s == 0 and deq:
                        dequant(it + 4, (it + 4) % 8, par)
                add_out(it)

            gate(0, 2)
            for part in range(2 * TT):
                norm_part(2, B - 1, part)
            gate(0, 3)
            for part in range(2 * TT, LN_PARTS):
                norm_part(2, B - 1, part)
            add_out(0)
            gate(1, 0)
            spread_tails(2, B - 1, 4)
            gate(1, 1)
            dequant(4, 4, 0)
            gate(1, 2)
            gate(1, 3)
            gate(2, 0)
            add_out(1)
            dequant(5, 5, 1)
            with dve.Fori(1, 14) as i2:
                iteration(2 * i2, 0, True, True)
                iteration(2 * i2 + 1, 1, True, True)
            with dve.Fori(28, 31) as it:
                iteration(it, 0, False, True)
            iteration(31, 1, False, False)


FAC_STEPS = 2 * 6 + 9
GELU_A = 0.7978845608028654
GELU_B = 0.044715

_INS = ["x", "ctx_1024", "L0_attn_Wq", "L0_attn_Wk", "L0_attn_Wv", "L0_attn_Wo", "L0_xattn_Wq", "L0_xattn_bq",
        "L0_xattn_Wk", "L0_xattn_bk", "L0_ffn_gate_W_packed", "L0_ffn_gate_scales", "L0_ffn_up_W_packed",
        "L0_ffn_up_scales", "L0_ffn_down_W_packed", "L0_ffn_down_scales"]
_OUTS = [((4, 512, 512), "float32")]


def kernel(**inputs):
    import numpy as _np
    import concourse.bacc as _bacc
    from concourse import mybir as _mybir
    from concourse.bass_utils import run_bass_kernel_spmd as _run

    nc = _bacc.Bacc("TRN2", target_bir_lowering=False, num_devices=1)
    arrays, args = {}, []
    for name in _INS:
        a = _np.ascontiguousarray(inputs[name])
        arrays[f"in_{name}_dram"] = a
        args.append(nc.dram_tensor(f"in_{name}_dram", a.shape, _mybir.dt.from_np(a.dtype), kind="ExternalInput").ap())
    for i, (shape, dtype) in enumerate(_OUTS):
        dt = _mybir.dt.from_np(_np.dtype(dtype))
        args.append(nc.dram_tensor(f"out_{i}_dram", shape, dt, kind="ExternalOutput").ap())
    decoder_layer(nc, *args)
    r = _run(nc, [arrays], core_ids=[0])
    got = tuple(r.results[0][f"out_{i}_dram"] for i in range(len(_OUTS)))
    return got[0]
```
